# Optimizing a Trainium2 kernel written in Bass

```python
import numpy as np
import jax
import jax.numpy as jnp

def _softmax(x, axis=-1):
    return jax.nn.softmax(x, axis=axis)

def _gelu(x):
    return jax.nn.gelu(x, approximate=True)

def _silu(x):
    return jax.nn.silu(x)

def _sigmoid(x):
    return jax.nn.sigmoid(x)

def _layernorm(x, axis=-1, eps=1e-05):
    m = jnp.mean(x, axis=axis, keepdims=True)
    v = jnp.var(x, axis=axis, keepdims=True)
    return (x - m) / jnp.sqrt(v + eps)

def _scatter_add(tgt, idx, src, axis=0):
    return tgt.at[idx].add(src)

def _segment_sum(src, seg, n):
    return jax.ops.segment_sum(src, seg, n)
kernel_name = 'mk_xattn_seq_d1_seqx_r4_8824ba'

def setup_inputs(seed: int=0):
    np.random.seed(seed)
    _w = jnp.asarray

    def _rec_inputs():
        import jax
        import jax.numpy as jnp
        _rk = jax.random.key(seed)
        x = -0.000719 + 1.001 * jax.random.normal(jax.random.fold_in(_rk, 1), (8, 512, 320), jnp.float32)
        _lenS = 512 - jax.random.randint(jax.random.fold_in(_rk, 7), (8,), 0, max(1, 512 // 4) + 1, jnp.int32)
        _lenS2 = 64 - jax.random.randint(jax.random.fold_in(_rk, 8), (8,), 0, max(1, 64 // 4) + 1, jnp.int32)
        _ctx_2048P = jax.random.normal(jax.random.fold_in(_rk, 11), (8, 16, 512), jnp.float32)
        _ctx_2048c = jax.random.dirichlet(jax.random.fold_in(_rk, 511), 0.3 * jnp.ones((16,), jnp.float32), (8, 64))
        _ctx_2048t = jnp.einsum('bsk,bkd->bsd', _ctx_2048c, _ctx_2048P)
        _ctx_2048t = _ctx_2048t * jax.lax.rsqrt(jnp.mean(jnp.square(_ctx_2048t)) + 1e-12) * 0.953939
        ctx_2048 = 0.00257118 + 0.99863 * (_ctx_2048t + 0.3 * jax.random.normal(jax.random.fold_in(_rk, 611), (8, 64, 512), jnp.float32))
        fside_S_0 = jax.random.uniform(jax.random.fold_in(_rk, 12), (512,), jnp.float32, 0.0, 0.999706)
        return (x, ctx_2048, fside_S_0)
    x, ctx_2048, fside_S_0 = _rec_inputs()

    def _L0_xattn_setup():
        import jax, jax.numpy as jnp
        import numpy as np
        HEADS = 20
        NUM_TOKENS = 4
        IP_SCALE = 1.0
        SEM_SCALE = 0.5
        RESCALE = 1.0
        EPS = 1e-12

        def _l2norm(x, axis=-1):
            n = jnp.sqrt(jnp.sum(x * x, axis=axis, keepdims=True))
            return x / jnp.maximum(n, EPS)
        key = jax.random.key(seed)
        ks = jax.random.split(key, 10)
        B, S, C = (2, 256, 320)
        T, E = (81, 512)
        inp = {'hidden_states': jax.random.normal(ks[0], (B, S, C), jnp.float32), 'encoder_hidden_states': jax.random.normal(ks[1], (B, T, E), jnp.float32), 'spatial_mask': jax.random.uniform(ks[2], (S,), jnp.float32), 'W_q': jax.random.normal(ks[3], (C, C), jnp.float32) * C ** (-0.5), 'W_k': jax.random.normal(ks[4], (E, C), jnp.float32) * E ** (-0.5), 'W_v': jax.random.normal(ks[5], (E, C), jnp.float32) * E ** (-0.5), 'W_k_ip': jax.random.normal(ks[6], (E, C), jnp.float32) * E ** (-0.5), 'W_v_ip': jax.random.normal(ks[7], (E, C), jnp.float32) * E ** (-0.5), 'W_out': jax.random.normal(ks[8], (C, C), jnp.float32) * C ** (-0.5), 'b_out': jnp.zeros((C,), jnp.float32)}
        return inp
    _L0_xattn_all = _L0_xattn_setup()
    _L0_xattn_in = {k: v for k, v in _L0_xattn_all.items() if k in ('W_q', 'W_k', 'W_v', 'W_k_ip', 'W_v_ip', 'W_out', 'b_out')}
    del _L0_xattn_all
    return {'x': x, 'ctx_2048': ctx_2048, 'fside_S_0': fside_S_0, 'L0_xattn_W_q': _L0_xattn_in['W_q'], 'L0_xattn_W_k': _L0_xattn_in['W_k'], 'L0_xattn_W_v': _L0_xattn_in['W_v'], 'L0_xattn_W_k_ip': _L0_xattn_in['W_k_ip'], 'L0_xattn_W_v_ip': _L0_xattn_in['W_v_ip'], 'L0_xattn_W_out': _L0_xattn_in['W_out'], 'L0_xattn_b_out': _L0_xattn_in['b_out']}

def reference(x, ctx_2048, fside_S_0, L0_xattn_W_q, L0_xattn_W_k, L0_xattn_W_v, L0_xattn_W_k_ip, L0_xattn_W_v_ip, L0_xattn_W_out, L0_xattn_b_out):
    import jax
    import jax.numpy as jnp

    def _L0_xattn_ref(hidden_states, encoder_hidden_states, spatial_mask, W_q, W_k, W_v, W_k_ip, W_v_ip, W_out, b_out):
        import jax, jax.numpy as jnp
        import numpy as np
        HEADS = 20
        NUM_TOKENS = 4
        IP_SCALE = 1.0
        SEM_SCALE = 0.5
        RESCALE = 1.0
        EPS = 1e-12

        def _l2norm(x, axis=-1):
            n = jnp.sqrt(jnp.sum(x * x, axis=axis, keepdims=True))
            return x / jnp.maximum(n, EPS)
        B, S, C = hidden_states.shape
        H = HEADS
        Dh = C // H
        attn_scale = Dh ** (-0.5)
        residual = hidden_states
        text_ehs = encoder_hidden_states[:, :-NUM_TOKENS]
        ip_ehs = encoder_hidden_states[:, -NUM_TOKENS:]

        def heads(x):
            return x.reshape(B, -1, H, Dh).transpose(0, 2, 1, 3)
        q = heads(hidden_states @ W_q)
        k_t = heads(text_ehs @ W_k)
        v_t = heads(text_ehs @ W_v)
        scores_t = jnp.einsum('bhsd,bhtd->bhst', q, k_t) * attn_scale
        probs_t = jax.nn.softmax(scores_t, axis=-1)
        text_out = jnp.einsum('bhst,bhtd->bhsd', probs_t, v_t)
        text_out = text_out.transpose(0, 2, 1, 3).reshape(B, S, C)
        k_ip = heads(ip_ehs @ W_k_ip)
        v_ip = heads(ip_ehs @ W_v_ip)
        attn_scores = jnp.einsum('bhsd,bhnd->bhsn', q, k_ip) * attn_scale
        qsem = jnp.einsum('bhst,bte->bhse', probs_t, text_ehs)
        qsem = _l2norm(qsem)
        ip_n = _l2norm(ip_ehs)
        sem = jnp.einsum('bhse,bne->bhsn', qsem, ip_n)
        sem = jax.lax.stop_gradient(sem)
        fused = attn_scores + SEM_SCALE * sem
        probs_ip = jax.nn.softmax(fused, axis=-1)
        probs_ip = probs_ip * spatial_mask[None, None, :, None]
        ip_out = jnp.einsum('bhsn,bhnd->bhsd', probs_ip, v_ip)
        ip_out = ip_out.transpose(0, 2, 1, 3).reshape(B, S, C)
        out = text_out + IP_SCALE * ip_out
        out = out @ W_out + b_out
        out = out + residual
        return out / RESCALE
    x = _L0_xattn_ref(x, ctx_2048, fside_S_0, L0_xattn_W_q, L0_xattn_W_k, L0_xattn_W_v, L0_xattn_W_k_ip, L0_xattn_W_v_ip, L0_xattn_W_out, L0_xattn_b_out)
    return x

_drawn_inputs = setup_inputs


def setup_inputs(seed=0):
    import zlib

    import numpy as np

    out = dict(_drawn_inputs(seed))
    spreads = {'L0_xattn_b_out': (0.0, 0.1)}
    factors = {}
    for name, (base, spread) in spreads.items():
        noise = np.random.default_rng([zlib.crc32(name.encode()), seed]).standard_normal(out[name].shape)
        drawn = base * np.exp(spread * noise) if base else spread * noise
        out[name] = jnp.asarray(drawn.astype(out[name].dtype))
    for name, factor in factors.items():
        out[name] = (out[name] * factor).astype(out[name].dtype)
    return out
```

```python
from contextlib import ExitStack

import concourse.bass as bass
from concourse import mybir

F32 = mybir.dt.float32
F32R = mybir.dt.float32r
ALU = mybir.AluOpType
ACT = mybir.ActivationFunctionType
AX_X = mybir.AxisListType.X

P = 128
HEADS = 20
NIP = 4
SEM_SCALE = 0.5
EPS = 1e-12
GROUP = 4
DMA = 16


class Batch:

    def __init__(self, number=None, step=None, place=0):
        self.number, self.step, self.place = number, step, place
        self.parity = (number if step is None else 1 + place) % 2

    def count(self, per_batch, extra):
        if self.step is None:
            return self.number * per_batch + extra
        return self.step * (2 * per_batch) + ((1 + self.place) * per_batch + extra)

    def has(self, per_batch, extra, end):
        return self.step is not None or 0 <= self.number * per_batch + extra < end

    def slot(self, per_batch, extra, ring):
        if self.step is None:
            return (self.number * per_batch + extra) % ring, (self.number * per_batch + extra) // ring
        at = (1 + self.place) * per_batch + extra
        return at % ring, self.step * (2 * per_batch // ring) + at // ring


def xattn_kernel(nc, x, ctx_tokens, ip_mask, w_q, w_k, w_v, w_k_ip, w_v_ip, w_out, b_out, out):
    B, S, C = x.shape
    _, TOK, E = ctx_tokens.shape
    T = TOK - NIP
    D = C // HEADS
    SCALE = D ** -0.5
    TILES = S // P
    HALVES = TILES // 2
    HALF = 2 * P
    GROUPS = HEADS // GROUP
    UNITS = TILES * GROUPS
    GROWS = GROUP * D
    EC = E // P
    QC = -(-C // P)
    QROWS = [min(P, C - P * m) for m in range(QC)]
    PAIRS = B // 2
    TABW = TOK + D + 1
    FINW = NIP + D + 1
    ALL_UNITS, ALL_TILES, ALL_HALVES = B * UNITS, B * TILES, B * HALVES
    XRING, YRING, SRING = 4, TILES, TILES
    ERING, TRING = 5, 4
    SLEAD, LEAD, TLEAD = 4, 3, 2
    HPC = P // D
    IPROWS = HEADS * NIP
    KM_STEPS, GV_STEPS = GROUPS, 6
    assert TOK * 2 == P and C == 2 * P + 64 and GROWS * 2 == P and B == 8 and TILES == 4

    es = ExitStack()
    with es:
        def sb(name, shape, dt=F32):
            return es.enter_context(nc.sbuf_tensor(name, shape, dt))

        def pb(name, shape):
            return es.enter_context(nc.psum_tensor(name, shape, F32))

        def sem(name):
            return es.enter_context(nc.semaphore(name))

        ctx_nat = sb("ctx_nat", [P, PAIRS, E])
        ip_nat = sb("ip_nat", [B * NIP, E])
        wk = sb("wk", [P, EC, C])
        wv = sb("wv", [P, EC, C])
        wkip = sb("wkip", [P, EC, C])
        wvip = sb("wvip", [P, EC, C])
        wq_nat = sb("wq_nat", [P, QC, C])
        wq_hi = sb("wq_hi", [P, QC, C], F32R)
        wq_lo = sb("wq_lo", [P, QC, C], F32R)
        wo = sb("wo", [P, QC, C])
        bias_all = sb("bias_all", [P, C])
        mask_sb = sb("mask_sb", [P, TILES])
        x_nat = sb("x_nat", [P, XRING, 2, C])
        ident = sb("ident", [P, P])
        head_of_row = sb("head_of_row", [P, HPC])
        group_mask = sb("group_mask", [P, GROUP])
        neg_half = sb("neg_half", [P, HEADS])
        ctxT = sb("ctxT", [P, EC, B * TOK])
        ctxM = sb("ctxM", [P, EC, B * TOK])
        ipn = sb("ipn", [B * NIP, E])
        ip_sq = sb("ip_sq", [B * NIP, E])
        ip_ss = sb("ip_ss", [B * NIP, 1])
        ip_ssc = sb("ip_ssc", [B * NIP, 1])
        ip_rn = sb("ip_rn", [B * NIP, 1])
        ktok = sb("ktok", [P, 2, GROUPS, B * TOK], F32R)
        g_sb = sb("g_sb", [P, PAIRS, TOK])
        v_sb = sb("v_sb", [P, PAIRS, C])
        vip_bd = sb("vip_bd", [P, QC, B * HPC * NIP])
        u_sb = sb("u_sb", [P, 5, C])
        u_all = sb("u_all", [IPROWS, B, C])
        km = sb("km", [P, 2, GROUPS, 2, GROUP * TOK], F32R)
        tab = sb("tab", [P, 2, HEADS, TABW])
        xh = sb("xh", [P, QC, HALF], F32R)
        xl = sb("xl", [P, QC - 1, HALF], F32R)
        qs = sb("qs", [P, 2, GROUPS, HALF], F32R)
        negmax = sb("negmax", [P, ERING, GROUP])
        e_sb = sb("e_sb", [P, ERING, GROUP * TOK])
        eT = sb("eT", [P, TRING, 2 * P])
        junk = sb("junk", [P, 2, GROUP, TOK])
        quad = sb("quad", [P, 2, HEADS])
        sip = sb("sip", [P, SRING, HEADS, NIP])
        fin = sb("fin", [P, 2, HEADS, FINW])
        guard = sb("guard", [P, 2, HEADS])
        quadc = sb("quadc", [P, 2, HEADS])
        rsum = sb("rsum", [P, 2, HEADS])
        lnq = sb("lnq", [P, 2, HEADS])
        rnorm = sb("rnorm", [P, 2, HEADS])
        semn = sb("semn", [P, 2, HEADS, NIP])
        fused = sb("fused", [P, 2, HEADS, NIP])
        ipmax = sb("ipmax", [P, 2, HEADS])
        ipd = sb("ipd", [P, 2, HEADS, NIP])
        ipe = sb("ipe", [P, 2, HEADS, NIP])
        ipsum = sb("ipsum", [P, 2, HEADS])
        iprec = sb("iprec", [P, 2, HEADS])
        ipw = sb("ipw", [P, 2, HEADS])
        pip = sb("pip", [P, 2, HEADS, NIP])
        attn = sb("attn", [P, 2, C])
        attnT = sb("attnT", [P, 4 * P])
        y_sb = sb("y_sb", [P, YRING, C])

        sc_ps = pb("sc_ps", [P, 2, 512])
        et_ps = pb("et_ps", [P, 2, 512])
        gv_ps = pb("gv_ps", [P, 2, 512])
        mi_ps = pb("mi_ps", [P, 2, 512])
        BANKS = [sc_ps[:, 0, :], sc_ps[:, 1, :], et_ps[:, 0, :], et_ps[:, 1, :], gv_ps[:, 0, :], gv_ps[:, 1, :]]

        in_ctx, in_wk, in_wq, in_wv = sem("in_ctx"), sem("in_wk"), sem("in_wq"), sem("in_wv")
        in_wkip, in_wvip, in_wo, in_ip = sem("in_wkip"), sem("in_wvip"), sem("in_wo"), sem("in_ip")
        in_bias, in_mask = sem("in_bias"), sem("in_mask")
        in_x = [sem(f"in_x{n}") for n in range(XRING)]
        y_stored = [sem(f"y_stored{n}") for n in range(YRING)]
        consts_step, ident_made, consts_made, zeros_made = (
            sem("consts_step"), sem("ident_made"), sem("consts_made"), sem("zeros_made"))
        pre_ctxT, pre_k, pre_v, pre_ipn, pre_g, pre_vip, pre_u = (
            sem(f"pre_{n}") for n in ("ctxT", "k", "v", "ipn", "g", "vip", "u"))
        ctxT_act, ctxT_dve, ctxM_made = sem("ctxT_act"), sem("ctxT_dve"), sem("ctxM_made")
        ip_step, ip_rn_made, ipn_made = sem("ip_step"), sem("ip_rn_made"), sem("ipn_made")
        k_hi, k_lo, v_copied, g_copied, vip_made = (
            sem("k_hi"), sem("k_lo"), sem("v_copied"), sem("g_copied"), sem("vip_made"))
        u_copied, u_placed, wq_hi_made, wq_lo_made = (
            sem("u_copied"), sem("u_placed"), sem("wq_hi_made"), sem("wq_lo_made"))
        xT_done, xT_hi, xT_lo = sem("xT_done"), sem("xT_hi"), sem("xT_lo")
        q_done, q_hi, q_lo = sem("q_done"), sem("q_hi"), sem("q_lo")
        xb_made = sem("xb_made")
        pool_turn = sem("pool_turn")
        km_made, tab_made = sem("km_made"), sem("tab_made")
        scores_done, max_done, exp_done = sem("scores_done"), sem("max_done"), sem("exp_done")
        eT_done, eT_copied = sem("eT_done"), sem("eT_copied")
        gv_done, quad_done, fin_copied = sem("gv_done"), sem("quad_done"), sem("fin_copied")
        guard_made, quadc_made, rsum_made = sem("guard_made"), sem("quadc_made"), sem("rsum_made")
        lnq_made = sem("lnq_made")
        rnorm_made, semn_made, fused_made = sem("rnorm_made"), sem("semn_made"), sem("fused_made")
        attn_made, ipmax_made, ipd_made, ipe_made = (
            sem("attn_made"), sem("ipmax_made"), sem("ipd_made"), sem("ipe_made"))
        ipsum_made, iprec_made, ipw_made, pip_made = (
            sem("ipsum_made"), sem("iprec_made"), sem("ipw_made"), sem("pip_made"))
        attnT_done, attnT_copied, out_done, y_made = (
            sem("attnT_done"), sem("attnT_copied"), sem("out_done"), sem("y_made"))

        x_t = x.rearrange("b (t p) c -> (b t) p c", p=P)
        out_t = out.rearrange("b (t p) c -> (b t) p c", p=P)

        def x_half(half):
            return x.rearrange("b (h t p) c -> (b h) p t c", p=P, t=2)[half]

        MISC_SLOTS = {0: ("x", 0), 1: ("o", 1), 2: ("x", 1), 3: ("q", 0), 4: ("at", 0),
                      5: ("q", 1), 6: ("o", 0), 8: ("q", 2), 9: ("at", 1)}
        MISC_ORDER = list(MISC_SLOTS.values())
        TASK_TILE = {("o", 1): -3, ("at", 0): -2, ("o", 0): -2, ("at", 1): -1}
        FIRST_BANK = {("x", 0): 0, ("x", 1): 1, ("q", 0): 0, ("q", 1): 1, ("q", 2): 0}

        def misc_bank(batch, half, kind, n):
            if batch.number == 0 and half == -1:
                return FIRST_BANK[kind, n]
            return (9 * half + MISC_ORDER.index((kind, n))) % 2

        def bank_released(batch, half, kind, n):
            if batch.number == 0 and half == -1:
                return (q_lo, 1) if (kind, n) == ("q", 2) else None
            at = 9 * half + MISC_ORDER.index((kind, n)) - 2
            while True:
                hh, (k, m) = at // 9, MISC_ORDER[at % 9]
                if k in "xq":
                    if batch.has(HALVES, hh + 1, ALL_HALVES):
                        if k == "x":
                            return xT_lo, batch.count(2 * HALVES, 2 * (hh + 1) + m + 1)
                        return q_lo, batch.count(3 * HALVES, 3 * (hh + 1) + m + 1)
                else:
                    t = 2 * hh + TASK_TILE[k, m]
                    if batch.has(TILES, t, ALL_TILES):
                        return (attnT_copied if k == "at" else y_made), batch.count(TILES, t + 1)
                at -= 2
                if batch.step is None and 2 * batch.number + at // 9 < -1:
                    return None

        def misc_task(batch, at):
            h, hu = divmod(at, UNITS // HALVES)
            kind, n = MISC_SLOTS.get(hu, ("", 0))
            if kind in ("x", "q") and batch.has(HALVES, h + 1, ALL_HALVES):
                return kind, n, h, None
            if kind in ("at", "o") and batch.has(TILES, 2 * h + TASK_TILE[kind, n], ALL_TILES):
                return kind, n, h, 2 * h + TASK_TILE[kind, n]
            return "", 0, 0, None

        LOOP_STEPS = (B - 2) // 2

        def run_batches(eng, first, body, last):
            first(Batch(0))
            with eng.Fori(0, LOOP_STEPS) as step:
                for place in range(2):
                    body(Batch(step=step, place=place))
            body(Batch(B - 1))
            last(Batch(B))

        block = es.enter_context(nc.Block())

        @block.sync
        def _(sp):
            ctx_pairs = ctx_tokens.rearrange("(q b) t e -> (b t) q e", b=2)
            for q in range(PAIRS):
                sp.dma_start(ctx_nat[:, q, :], ctx_tokens.rearrange("(q b) t e -> q (b t) e", b=2)[q]).then_inc(in_ctx, DMA)
            sp.dma_start(wk[:], w_k.rearrange("(c p) n -> p c n", p=P)).then_inc(in_wk, DMA)
            sp.dma_start(x_nat[:, 0], x_half(0)).then_inc(in_x[0], DMA)
            sp.dma_start(wv[:], w_v.rearrange("(c p) n -> p c n", p=P)).then_inc(in_wv, DMA)
            sp.dma_start(bias_all[:], b_out.rearrange("(a c) -> a c", a=1).to_broadcast([P, C])).then_inc(in_bias, DMA)
            sp.dma_start(wvip[:], w_v_ip.rearrange("(c p) n -> p c n", p=P)).then_inc(in_wvip, DMA)
            for half in range(1, XRING):
                sp.dma_start(x_nat[:, half], x_half(half)).then_inc(in_x[half], DMA)
            sp.wait_ge(u_copied, 5)
            for b in range(B):
                for m in range(2):
                    r, blk = 32 * (b % 4), 2 * m + b // 4
                    sp.dma_start(u_all[32 * m:32 * m + 32, b, :], u_sb[r:r + 32, blk, :]).then_inc(u_placed, DMA)
                sp.dma_start(u_all[64:80, b, :], u_sb[16 * b:16 * b + 16, 4, :]).then_inc(u_placed, DMA)

            def store(batch, s):
                sp.wait_ge(y_made, batch.count(TILES, s + 1))
                sp.dma_start(out_t[batch.count(TILES, s)], y_sb[:, s]).then_inc(y_stored[s], DMA)

            def stores_and_loads(batch, number):
                for h in range(HALVES):
                    store(batch, 2 * h)
                    store(batch, 2 * h + 1)
                    if number is None or number < B - 2:
                        slot, _ = batch.slot(HALVES, h, XRING)
                        sp.dma_start(x_nat[:, slot], x_half(batch.count(HALVES, h + XRING))).then_inc(in_x[slot], DMA)

            stores_and_loads(Batch(0), 0)
            with sp.Fori(0, LOOP_STEPS - 1) as step:
                for place in range(2):
                    stores_and_loads(Batch(step=step, place=place), None)
            for number in range(B - 3, B):
                stores_and_loads(Batch(number), number)
            for s in range(YRING):
                sp.wait_ge(y_stored[s], DMA * (B + 1))

        @block.gpsimd
        def _(pool):
            g = nc.gpsimd
            g.memset(ident[:], 0.0).then_inc(consts_step, 1)
            pool.wait_ge(consts_step, 1)
            g.affine_select(out=ident[:], in_=ident[:], compare_op=ALU.not_equal, fill=1.0, base=0,
                            pattern=[[-1, P]], channel_multiplier=1).then_inc(ident_made, 1)
            g.memset(head_of_row[:], 1.0).then_inc(consts_step, 1)
            pool.wait_ge(consts_step, 2)
            g.affine_select(out=head_of_row[:], in_=head_of_row[:], compare_op=ALU.is_ge, fill=0.0, base=0,
                            pattern=[[-D, HPC]], channel_multiplier=1).then_inc(consts_step, 1)
            pool.wait_ge(consts_step, 3)
            g.affine_select(out=head_of_row[:], in_=head_of_row[:], compare_op=ALU.is_ge, fill=0.0, base=D - 1,
                            pattern=[[D, HPC]], channel_multiplier=-1).then_inc(consts_step, 1)
            pool.wait_ge(consts_step, 4)
            g.tensor_copy(group_mask[0:64], head_of_row[0:64, 0:GROUP]).then_inc(consts_made, 1)
            pool.wait_ge(consts_made, 1)
            g.tensor_copy(group_mask[64:P], head_of_row[64:P, GROUP:HPC]).then_inc(consts_made, 1)
            pool.wait_ge(consts_made, 2)
            g.memset(neg_half[:], -0.5).then_inc(consts_made, 1)
            g.memset(e_sb[:].rearrange("p r (h t) -> p (r h) t", t=TOK)[:, :, T:TOK], 0.0).then_inc(zeros_made, 1)
            pool.wait_ge(consts_made, 3)
            pool.wait_ge(ip_step, 2)
            g.tensor_tensor(ip_rn[:], ip_ssc[:], neg_half[0:B * NIP, 0:1], ALU.pow).then_inc(ip_rn_made, 1)
            pool.wait_ge(zeros_made, 2)
            pool.wait_ge(ip_rn_made, 1)
            for par in range(2):
                for r in range(2):
                    g.memset(tab[64 * r:64 * r + T, par, r::2, TABW - 1:TABW], 1.0).then_inc(zeros_made, 1)
                    pool.wait_ge(zeros_made, 3 + 2 * par + r)

            def km_step(batch, c):
                cols = batch.count(TOK, 0)
                g.tensor_tensor(
                    km[:, batch.parity, c].rearrange("p s (j t) -> p s j t", t=TOK),
                    ktok[:, :, c, bass.ds(cols, TOK)].unsqueeze(2).to_broadcast([P, 2, GROUP, TOK]),
                    group_mask[:].unsqueeze(1).unsqueeze(3).to_broadcast([P, 2, GROUP, TOK]),
                    ALU.mult).then_inc(km_made, 1)

            def tab_step(batch, n):
                r = n % 2
                _, pair = batch.slot(1, 0, 2)
                src = 64 * batch.parity
                rows = slice(64 * r, 64 * r + T)
                if n < 4:
                    h0 = 10 * (n // 2) + r
                    g.tensor_copy(tab[rows, batch.parity, h0:h0 + 9:2, 0:TOK],
                                  g_sb[src:src + T, pair, :].unsqueeze(1).to_broadcast([T, 5, TOK])
                                  if isinstance(pair, int) else
                                  g_sb[src:src + T, bass.ds(pair, 1), :].to_broadcast([T, 5, TOK])).then_inc(tab_made, 1)
                else:
                    v = v_sb[src:src + T, bass.ds(pair, 1), :].rearrange("p a (h d) -> p (a h) d", d=D)
                    g.tensor_copy(tab[rows, batch.parity, r::2, TOK:TOK + D], v[:, r::2, :]).then_inc(tab_made, 1)
                pool.wait_ge(tab_made, batch.count(GV_STEPS, n + 1))
                pool.sem_inc(pool_turn, 1)

            def add_bias(batch, half):
                slot, _ = batch.slot(HALVES, half, XRING)
                pool.wait_ge(xT_done, batch.count(2 * HALVES, 2 * half + 2))
                g.tensor_tensor(x_nat[:, slot], x_nat[:, slot],
                                bias_all[:].unsqueeze(1).to_broadcast([P, 2, C]), ALU.add).then_inc(xb_made, 1)

            pool.wait_ge(k_hi, 2 * GROUPS)
            pool.wait_ge(k_lo, 2 * GROUPS)
            for c in range(GROUPS):
                km_step(Batch(0), c)
            pool.wait_ge(g_copied, 2)
            pool.wait_ge(v_copied, PAIRS)
            pool.wait_ge(zeros_made, 6)
            pool.wait_ge(km_made, KM_STEPS)
            for n in range(GV_STEPS):
                tab_step(Batch(0), n)
            pool.wait_ge(in_bias, DMA)
            add_bias(Batch(0), 0)

            def nxt(batch):
                return (Batch(batch.number + 1) if batch.step is None else
                        Batch(step=batch.step, place=batch.place + 1))

            def builds(batch, s, part):
                if not batch.has(1, 1, B):
                    return
                to = nxt(batch)
                k = 2 * s + part
                if k == 0 and batch.has(1, -1, B):
                    pool.wait_ge(scores_done, batch.count(UNITS, 0))
                    pool.wait_ge(gv_done, batch.count(UNITS, 0))
                for c in ((0,), (1,), (2,), (3,), (4,), (), (), ())[k]:
                    km_step(to, c)
                if k in (5, 7):
                    pool.wait_ge(fused_made, batch.count(TILES, s))
                    pool.sem_inc(pool_turn, 1)
                for n in ((), (), (), (), (), (0, 1), (2, 3), (4, 5))[k]:
                    tab_step(to, n)

            def tile(batch, s):
                builds(batch, s, 0)
                if batch.has(TILES, s - 1, ALL_TILES):
                    n, par = batch.count(TILES, s), (s - 1) % 2
                    pool.wait_ge(rsum_made, n)
                    g.tensor_tensor(attn[:, par].rearrange("p (h d) -> p h d", d=D), fin[:, par, :, NIP:NIP + D],
                                    rsum[:, par].unsqueeze(2).to_broadcast([P, HEADS, D]), ALU.mult).then_inc(attn_made, 1)
                if batch.has(TILES, s - 2, ALL_TILES):
                    par2 = s % 2
                    pool.wait_ge(ipw_made, batch.count(TILES, s - 1))
                    g.tensor_tensor(pip[:, par2], ipe[:, par2],
                                    ipw[:, par2].unsqueeze(2).to_broadcast([P, HEADS, NIP]), ALU.mult).then_inc(pip_made, 1)
                if batch.has(TILES, s - 1, ALL_TILES):
                    pool.wait_ge(rnorm_made, n)
                    g.tensor_tensor(semn[:, par], fin[:, par, :, 0:NIP],
                                    rnorm[:, par].unsqueeze(2).to_broadcast([P, HEADS, NIP]), ALU.mult).then_inc(semn_made, 1)
                    pool.wait_ge(semn_made, n)
                    g.tensor_tensor(fused[:, par], semn[:, par], sip[:, (s - 1) % SRING], ALU.add).then_inc(fused_made, 1)
                builds(batch, s, 1)
                if s % 2 == 1 and batch.has(HALVES, s // 2 + 1, ALL_HALVES):
                    add_bias(batch, s // 2 + 1)

            def body(batch):
                for s in range(TILES):
                    tile(batch, s)

            def drain(batch):
                for s in range(2):
                    tile(batch, s)

            run_batches(pool, body, body, drain)

        @block.scalar
        def _(act):
            nc.scalar.preload_act_table_set("natural_log_exp_and_others")
            act.dma_start(wq_nat[:, 0:QC - 1], w_q[0:2 * P, :].rearrange("(c p) n -> p c n", p=P)).then_inc(in_wq, DMA)
            act.dma_start(wq_nat[0:64, QC - 1], w_q[2 * P:C, :]).then_inc(in_wq, DMA)
            act.dma_start(wq_nat[64:P, QC - 1], w_q[2 * P:C, :]).then_inc(in_wq, DMA)
            act.dma_start(ip_nat[:], ctx_tokens[:, T:TOK, :]).then_inc(in_ip, DMA)
            act.dma_start(wkip[:], w_k_ip.rearrange("(c p) n -> p c n", p=P)).then_inc(in_wkip, DMA)
            act.dma_start(mask_sb[:], ip_mask.rearrange("(t p) -> p t", p=P)).then_inc(in_mask, DMA)
            act.dma_start(wo[:, 0:QC - 1], w_out[0:2 * P, :].rearrange("(c p) n -> p c n", p=P)).then_inc(in_wo, DMA)
            act.dma_start(wo[0:64, QC - 1], w_out[2 * P:C, :]).then_inc(in_wo, DMA)

            def x_hi(batch, half, n):
                act.wait_ge(xT_done, batch.count(2 * HALVES, 2 * half + n + 1))
                ps = mi_ps[:, misc_bank(batch, half - 1, "x", n), :]
                if n == 0:
                    nc.scalar.copy(xh[:, 0:2, :], ps.rearrange("p (c t) -> p c t", c=2)).then_inc(xT_hi, 1)
                else:
                    nc.scalar.copy(xh[0:64, 2, :], ps[64:P, 0:HALF]).then_inc(xT_hi, 1)

            def q_high(batch, half, m):
                act.wait_ge(q_done, batch.count(3 * HALVES, 3 * half + m + 1))
                ps = mi_ps[:, misc_bank(batch, half - 1, "q", m), :]
                for a in range(QROWS[m] // 64):
                    last = nc.scalar.copy(qs[0:64, half % 2, 2 * m + a, :], ps[64 * a:64 * a + 64, 0:HALF])
                last.then_inc(q_hi, 1)

            def exps(batch, u):
                slot, bank = u % ERING, u % 2
                act.wait_ge(max_done, batch.count(UNITS, u + 1))
                for j in range(GROUP):
                    last = nc.scalar.activation(e_sb[:, slot, TOK * j:TOK * j + T], sc_ps[:, bank, TOK * j:TOK * j + T],
                                                ACT.Exp, bias=negmax[:, slot, j:j + 1])
                last.then_inc(exp_done, 1)

            def copy_fin(batch, u):
                s, c = divmod(u, GROUPS)
                act.wait_ge(quad_done, batch.count(UNITS, u + 1))
                ps = gv_ps[:, u % 2, 0:GROUP * TABW].rearrange("p (h w) -> p h w", w=TABW)
                nc.scalar.copy(fin[:, s % 2, GROUP * c:GROUP * c + GROUP, :], ps[:, :, TOK - NIP:TABW]).then_inc(fin_copied, 1)

            def copy_eT(batch, u):
                act.wait_ge(eT_done, batch.count(UNITS, u + 1))
                nc.scalar.copy(eT[:, u % TRING, :], et_ps[:, u % 2, 0:2 * P]).then_inc(eT_copied, 1)

            for q in (0, 2):
                act.wait_ge(pre_ctxT, q + 1)
                nc.scalar.copy(ctxT[:, :, P * q:P * q + P],
                               BANKS[q].rearrange("p (c t) -> p c t", c=EC)).then_inc(ctxT_act, 1)
            act.wait_ge(in_wq, 3 * DMA)
            nc.scalar.copy(wq_hi[:], wq_nat[:]).then_inc(wq_hi_made, 1)
            x_hi(Batch(0), 0, 0)
            x_hi(Batch(0), 0, 1)
            for m in range(QC):
                act.wait_ge(pre_k, m + 1)
                for a in range(QROWS[m] // 64):
                    for half in range(2):
                        nc.scalar.activation(ktok[64 * half:64 * half + 64, 0, 2 * m + a, :],
                                             BANKS[(4, 5, 0)[m]][64 * a:64 * a + 64, :], ACT.Copy, scale=SCALE).then_inc(k_hi, 1)
                if m > 0:
                    q_high(Batch(0), 0, m - 1)
            q_high(Batch(0), 0, 2)
            for q in range(PAIRS):
                act.wait_ge(pre_v, q + 1)
                nc.scalar.copy(v_sb[:, q, :], BANKS[1 + q][:, 0:C]).then_inc(v_copied, 1)
            for n in range(5):
                act.wait_ge(pre_u, n + 1)
                nc.scalar.copy(u_sb[:, n, :], BANKS[(2, 3, 4, 5, 2)[n]][:, 0:C]).then_inc(u_copied, 1)
            exps(Batch(0), 0)
            exps(Batch(0), 1)
            copy_eT(Batch(0), 0)
            exps(Batch(0), 2)
            copy_eT(Batch(0), 1)

            def slot(batch, u):
                s, j = divmod(u, GROUPS)
                before, par, n = batch.has(TILES, s - 1, ALL_TILES), (s - 1) % 2, batch.count(TILES, s)
                if batch.has(UNITS, u - 2, ALL_UNITS):
                    copy_fin(batch, u - 2)
                kind, m, h, t = misc_task(batch, u - 1)
                if kind == "x":
                    x_hi(batch, h + 1, m)
                if kind == "q":
                    q_high(batch, h + 1, m)
                if kind == "at":
                    act.wait_ge(attnT_done, batch.count(TILES, t + 1))
                    ps = mi_ps[:, misc_bank(batch, h, "at", m), :]
                    nc.scalar.copy(attnT[:, 0:2 * P], ps[:, 0:2 * P])
                    nc.scalar.copy(attnT[0:64, 2 * P:3 * P], ps[0:64, 2 * P:3 * P])
                    nc.scalar.copy(attnT[0:IPROWS, 3 * P:4 * P], ps[0:IPROWS, 3 * P:4 * P]).then_inc(attnT_copied, 1)
                if batch.has(UNITS, u + LEAD, ALL_UNITS):
                    exps(batch, u + LEAD)
                if j == 3 and before:
                    act.wait_ge(quadc_made, n)
                    nc.scalar.activation(lnq[:, par], quadc[:, par], ACT.Ln).then_inc(lnq_made, 1)
                if batch.has(UNITS, u + TLEAD, ALL_UNITS):
                    copy_eT(batch, u + TLEAD)
                if j == 3 and before:
                    act.wait_ge(lnq_made, n)
                    nc.scalar.activation(rnorm[:, par], lnq[:, par], ACT.Exp, scale=-0.5).then_inc(rnorm_made, 1)
                if j == 0 and batch.has(TILES, s - 2, ALL_TILES):
                    act.wait_ge(ipd_made, batch.count(TILES, s - 1))
                    nc.scalar.activation(ipe[:, s % 2], ipd[:, s % 2], ACT.Exp).then_inc(ipe_made, 1)

            def body(batch):
                for u in range(UNITS):
                    slot(batch, u)

            def drain(batch):
                for u in range(2 * GROUPS + 1):
                    slot(batch, u)

            run_batches(act, body, body, drain)

        @block.vector
        def _(dve):
            v = nc.vector
            v.memset(tab[:], 0.0).then_inc(zeros_made, 1)
            for place in range(YRING):
                dve.sem_inc(y_stored[place], DMA)

            def x_low(batch, half, n):
                dve.wait_ge(xT_hi, batch.count(2 * HALVES, 2 * half + n + 1))
                ps = mi_ps[:, misc_bank(batch, half - 1, "x", n), :]
                if n == 0:
                    v.tensor_tensor(xl[:], ps.rearrange("p (c t) -> p c t", c=2), xh[:, 0:2, :].bitcast(F32),
                                    ALU.subtract).then_inc(xT_lo, 1)
                else:
                    v.tensor_tensor(xh[64:P, 2, :], ps[64:P, 0:HALF], xh[0:64, 2, :].bitcast(F32),
                                    ALU.subtract).then_inc(xT_lo, 1)

            def q_low(batch, half, m):
                dve.wait_ge(q_hi, batch.count(3 * HALVES, 3 * half + m + 1))
                ps = mi_ps[:, misc_bank(batch, half - 1, "q", m), :]
                for a in range(QROWS[m] // 64):
                    c = 2 * m + a
                    last = v.tensor_tensor(qs[64:P, half % 2, c, :], ps[64 * a:64 * a + 64, 0:HALF],
                                           qs[0:64, half % 2, c, :].bitcast(F32), ALU.subtract)
                last.then_inc(q_lo, 1)

            def maxima(batch, u):
                s, c = divmod(u % UNITS, GROUPS)
                dve.wait_ge(scores_done, batch.count(UNITS, u + 1))
                ps = sc_ps[:, u % 2, 0:GROUP * TOK].rearrange("p (h t) -> p h t", t=TOK)
                v.tensor_copy(sip[:, s % SRING, GROUP * c:GROUP * c + GROUP, :], ps[:, :, T:TOK])
                v.tensor_reduce(negmax[:, u % ERING, :], ps[:, :, 0:T], AX_X, ALU.max, negate=True).then_inc(max_done, 1)

            def quadratic(batch, u):
                s, c = divmod(u, GROUPS)
                dve.wait_ge(gv_done, batch.count(UNITS, u + 1))
                for j in range(GROUP):
                    h = GROUP * c + j
                    last = v.tensor_tensor_reduce(
                        out=junk[:, u % 2, j, 0:T], in0=gv_ps[:, u % 2, TABW * j:TABW * j + T],
                        in1=e_sb[:, u % ERING, TOK * j:TOK * j + T], scale=1.0, scalar=0.0,
                        op0=ALU.mult, op1=ALU.add, accum_out=quad[:, s % 2, h:h + 1])
                last.then_inc(quad_done, 1)

            dve.wait_ge(in_ip, DMA)
            v.tensor_tensor_reduce(out=ip_sq[:], in0=ip_nat[:], in1=ip_nat[:], scale=1.0, scalar=0.0,
                                   op0=ALU.mult, op1=ALU.add, accum_out=ip_ss[:]).then_inc(ip_step, 1)
            dve.wait_ge(ip_step, 1)
            v.tensor_scalar(ip_ssc[:], ip_ss[:], EPS * EPS, None, ALU.max).then_inc(ip_step, 1)
            for q in (1, 3):
                dve.wait_ge(pre_ctxT, q + 1)
                v.tensor_copy(ctxT[:, :, P * q:P * q + P], BANKS[q].rearrange("p (c t) -> p c t", c=EC)).then_inc(ctxT_dve, 1)
            dve.wait_ge(wq_hi_made, 1)
            v.tensor_tensor(wq_lo[:], wq_nat[:], wq_hi[:].bitcast(F32), ALU.subtract).then_inc(wq_lo_made, 1)
            dve.wait_ge(ip_rn_made, 1)
            v.tensor_scalar(ipn[:], ip_nat[:], ip_rn[:], SEM_SCALE, ALU.mult, ALU.mult).then_inc(ipn_made, 1)
            x_low(Batch(0), 0, 0)
            x_low(Batch(0), 0, 1)
            for m in range(QC):
                for a in range(QROWS[m] // 64):
                    for half in range(2):
                        c = 2 * m + a
                        dve.wait_ge(k_hi, 2 * c + 2)
                        v.scalar_tensor_tensor(out=ktok[64 * half:64 * half + 64, 1, c, :],
                                               in0=BANKS[(4, 5, 0)[m]][64 * a:64 * a + 64, :], scalar=SCALE,
                                               in1=ktok[64 * half:64 * half + 64, 0, c, :].bitcast(F32),
                                               op0=ALU.mult, op1=ALU.subtract).then_inc(k_lo, 1)
                if m > 0:
                    q_low(Batch(0), 0, m - 1)
            q_low(Batch(0), 0, 2)
            dve.wait_ge(ctxT_act, 2)
            dve.wait_ge(ctxT_dve, 2)
            v.tensor_copy(ctxM[:].rearrange("p c (b t) -> p (c b) t", t=TOK)[:, :, 0:T],
                          ctxT[:].rearrange("p c (b t) -> p (c b) t", t=TOK)[:, :, 0:T]).then_inc(ctxM_made, 1)
            dve.wait_ge(pre_ipn, 1)
            v.tensor_copy(ctxM[:].rearrange("p c (b t) -> p (c b) t", t=TOK)[:, :, T:TOK],
                          BANKS[5][:, 0:EC * B * NIP].rearrange("p (c n) -> p c n", n=NIP)).then_inc(ctxM_made, 1)
            dve.wait_ge(pre_vip, 1)
            for m in range(QC):
                hp = QROWS[m] // D
                rows = QROWS[m]
                v.tensor_tensor(
                    vip_bd[0:rows, m, 0:B * hp * NIP].rearrange("p (b h n) -> p b h n", h=hp, n=NIP),
                    BANKS[0][0:rows, 32 * m:32 * m + 32].rearrange("p (b n) -> p b n", n=NIP).unsqueeze(2)
                    .to_broadcast([rows, B, hp, NIP]),
                    head_of_row[0:rows, 0:hp].unsqueeze(1).unsqueeze(3).to_broadcast([rows, B, hp, NIP]),
                    ALU.mult).then_inc(vip_made, 1)
            dve.wait_ge(pre_g, 1)
            for r in range(2):
                v.tensor_copy(g_sb[64 * r:64 * r + 64],
                              BANKS[1][64 * r:64 * r + 64, :].rearrange("p (q t) -> p q t", q=PAIRS)[:, :, 64 * r:64 * r + 64]
                              ).then_inc(g_copied, 1)
            maxima(Batch(0), 0)
            maxima(Batch(0), 1)
            maxima(Batch(0), 2)
            dve.wait_ge(in_mask, DMA)

            def add_residual(batch, bank, t):
                slot, _ = batch.slot(HALVES, t // 2, XRING)
                dve.wait_ge(out_done, batch.count(TILES, t + 1))
                dve.wait_ge(xb_made, batch.count(HALVES, t // 2 + 1))
                if batch.has(TILES, t - YRING, ALL_TILES):
                    dve.wait_ge(y_stored[t % YRING], batch.count(DMA, DMA * (t // TILES + 1)))
                v.tensor_tensor(y_sb[:, t % YRING], mi_ps[:, bank, 0:C], x_nat[:, slot, t % 2], ALU.add).then_inc(y_made, 1)

            def slot(batch, u):
                s, j = divmod(u, GROUPS)
                par, n = (s - 1) % 2, batch.count(TILES, s)
                par2, n2 = s % 2, batch.count(TILES, s - 1)
                before, before2 = batch.has(TILES, s - 1, ALL_TILES), batch.has(TILES, s - 2, ALL_TILES)
                if batch.has(UNITS, u + LEAD, ALL_UNITS):
                    maxima(batch, u + LEAD)
                if j == 0 and before2:
                    dve.wait_ge(ipmax_made, n2)
                    v.tensor_tensor(ipd[:, par2], fused[:, par2], ipmax[:, par2].unsqueeze(2).to_broadcast([P, HEADS, NIP]),
                                    ALU.subtract).then_inc(ipd_made, 1)
                if j == 1 and before2:
                    dve.wait_ge(ipe_made, n2)
                    v.tensor_reduce(ipsum[:, par2], ipe[:, par2], AX_X, ALU.add).then_inc(ipsum_made, 1)
                if j == 2 and before2:
                    dve.wait_ge(ipsum_made, n2)
                    v.reciprocal(iprec[:, par2], ipsum[:, par2]).then_inc(iprec_made, 1)
                if j == 2 and before:
                    dve.wait_ge(fin_copied, batch.count(UNITS, GROUPS * s))
                    ssum = fin[:, par, :, FINW - 1]
                    v.reciprocal(rsum[:, par], ssum).then_inc(rsum_made, 1)
                    v.scalar_tensor_tensor(out=guard[:, par], in0=ssum, scalar=EPS * EPS, in1=ssum,
                                           op0=ALU.mult, op1=ALU.mult).then_inc(guard_made, 1)
                kind, m, h, t = misc_task(batch, u - 2)
                if kind == "o":
                    add_residual(batch, misc_bank(batch, h, "o", m), t)
                if batch.has(UNITS, u - 1, ALL_UNITS):
                    quadratic(batch, u - 1)
                if j == 2 and before2:
                    dve.wait_ge(iprec_made, n2)
                    st = (s - 2) % TILES
                    v.tensor_scalar(ipw[:, par2], iprec[:, par2], mask_sb[:, st:st + 1], None, ALU.mult).then_inc(ipw_made, 1)
                if j == 2 and before:
                    dve.wait_ge(guard_made, n)
                    v.tensor_tensor(quadc[:, par], quad[:, par], guard[:, par], ALU.max).then_inc(quadc_made, 1)
                if j == 4 and before:
                    dve.wait_ge(fused_made, n)
                    v.tensor_reduce(ipmax[:, par], fused[:, par], AX_X, ALU.max).then_inc(ipmax_made, 1)
                kind, m, h, _ = misc_task(batch, u - 1)
                if kind == "x":
                    x_low(batch, h + 1, m)
                if kind == "q":
                    q_low(batch, h + 1, m)

            def body(batch):
                for u in range(UNITS):
                    slot(batch, u)

            def drain(batch):
                for u in range(3 * GROUPS - 1):
                    slot(batch, u)

            run_batches(dve, body, body, drain)

        @block.tensor
        def _(pe):
            mm, tr = nc.tensor.matmul, nc.tensor.transpose

            def x_transposes(batch, half, n):
                slot, use = batch.slot(HALVES, half, XRING)
                if n == 0:
                    pe.wait_ge(in_x[slot], use * DMA + DMA)
                before = bank_released(batch, half - 1, "x", n)
                if before:
                    pe.wait_ge(*before)
                ps = mi_ps[:, misc_bank(batch, half - 1, "x", n), :]
                for t in range(2):
                    if n == 0:
                        for c in range(2):
                            last = tr(ps[:, HALF * c + P * t:HALF * c + P * t + P], x_nat[:, slot, t, P * c:P * c + P], ident[:])
                    else:
                        last = tr(ps[:, P * t:P * t + P], x_nat[:, slot, t, C - P:C], ident[:])
                last.then_inc(xT_done, 1)

            def q_project(batch, half, m):
                if m == 0:
                    pe.wait_ge(xT_lo, batch.count(2 * HALVES, 2 * half + 2))
                before = bank_released(batch, half - 1, "q", m)
                if before:
                    pe.wait_ge(*before)
                ps = mi_ps[0:QROWS[m], misc_bank(batch, half - 1, "q", m), 0:HALF]
                cols = slice(P * m, P * m + QROWS[m])
                steps = [(wq_hi[:, c, cols], xh[:, c, :]) for c in range(3)]
                steps += [(wq_lo[:, c, cols], xh[:, c, :]) for c in range(3)]
                steps += [(wq_hi[:, c, cols], xl[:, c, :]) for c in range(2)]
                for n, (w, xx) in enumerate(steps):
                    last = mm(ps, w, xx, start=n == 0, stop=n == len(steps) - 1)
                last.then_inc(q_done, 1)

            def scores(batch, u):
                of = batch
                s, c = divmod(u % UNITS, GROUPS)
                parity = (batch.parity + u // UNITS) % 2
                half = u // UNITS * HALVES + s // 2
                if batch.has(UNITS, u - 2, ALL_UNITS):
                    pe.wait_ge(exp_done, batch.count(UNITS, u - 1))
                if s == 0:
                    pe.wait_ge(km_made, batch.count(KM_STEPS, KM_STEPS * (u // UNITS) + c + 1))
                if s % 2 == 0 and c % 2 == 0:
                    pe.wait_ge(q_lo, batch.count(3 * HALVES, 3 * half + c // 2 + 1))
                q = qs[:, half % 2, c, P * (s % 2):P * (s % 2) + P]
                for part in range(2):
                    last = mm(sc_ps[:, u % 2, 0:GROUP * TOK], q, km[:, parity, c, part, :], start=part == 0, stop=part == 1)
                last.then_inc(scores_done, 1)

            def e_transposes(batch, u):
                pe.wait_ge(exp_done, batch.count(UNITS, u + 1))
                if batch.has(UNITS, u - 2, ALL_UNITS):
                    pe.wait_ge(eT_copied, batch.count(UNITS, u - 1))
                for r in range(2):
                    last = tr(et_ps[:, u % 2, P * r:P * r + P], e_sb[:, u % ERING, P * r:P * r + P], ident[:])
                last.then_inc(eT_done, 1)

            def table_products(batch, u):
                s, c = divmod(u, GROUPS)
                pe.wait_ge(eT_copied, batch.count(UNITS, u + 1))
                if batch.has(UNITS, u - 2, ALL_UNITS):
                    pe.wait_ge(fin_copied, batch.count(UNITS, u - 1))
                if u == 0:
                    pe.wait_ge(tab_made, batch.count(GV_STEPS, GV_STEPS))
                for r in range(2):
                    h = GROUP * c + 2 * r
                    last = mm(gv_ps[:, u % 2, 2 * TABW * r:2 * TABW * r + 2 * TABW], eT[:, u % TRING, P * r:P * r + P],
                              tab[:, batch.parity, h:h + 2, :].rearrange("p h w -> p (h w)"), start=True, stop=True)
                last.then_inc(gv_done, 1)

            def attn_transposes(batch, h, n, t):
                par = t % 2
                pe.wait_ge(attn_made, batch.count(TILES, t + 1))
                pe.wait_ge(pip_made, batch.count(TILES, t + 1))
                before = bank_released(batch, h, "at", n)
                if before:
                    pe.wait_ge(*before)
                ps = mi_ps[:, misc_bank(batch, h, "at", n), :]
                for c in range(QC):
                    tr(ps[0:QROWS[c], P * c:P * c + P], attn[:, par, P * c:P * c + QROWS[c]], ident[:])
                tr(ps[0:IPROWS, 3 * P:4 * P], pip[:, par].rearrange("p h n -> p (h n)"), ident[:]).then_inc(attnT_done, 1)

            def out_project(batch, h, n, t, part):
                ps = mi_ps[:, misc_bank(batch, h, "o", n), 0:C]
                if part == 0:
                    pe.wait_ge(attnT_copied, batch.count(TILES, t + 1))
                    before = bank_released(batch, h, "o", n)
                    if before:
                        pe.wait_ge(*before)
                    for c in range(2):
                        mm(ps, attnT[:, P * c:P * c + P], wo[:, c, :], start=c == 0, stop=False)
                else:
                    mm(ps, attnT[0:QROWS[2], 2 * P:3 * P], wo[0:QROWS[2], 2, :], start=False, stop=False)
                    mm(ps, attnT[0:IPROWS, 3 * P:4 * P], u_all[:, batch.count(1, t // TILES), :],
                       start=False, stop=True).then_inc(out_done, 1)

            pe.wait_ge(ident_made, 1)
            pe.wait_ge(in_ctx, PAIRS * DMA)
            for q in range(PAIRS):
                for c in range(EC):
                    last = tr(BANKS[q][:, P * c:P * c + P], ctx_nat[:, q, P * c:P * c + P], ident[:])
                last.then_inc(pre_ctxT, 1)
            x_transposes(Batch(0), 0, 0)
            x_transposes(Batch(0), 0, 1)
            by_batch = ctxT[:].rearrange("p c (b t) -> p c b t", t=TOK)
            pe.wait_ge(ctxT_act, 2)
            pe.wait_ge(ctxT_dve, 2)
            pe.wait_ge(in_wk, DMA)
            pe.wait_ge(in_wkip, DMA)
            for m in range(QC):
                ps = BANKS[(4, 5, 0)[m]][0:QROWS[m], :].rearrange("p (b t) -> p b t", t=TOK)
                for c in range(EC):
                    mm(ps[:, :, 0:T], wk[:, c, P * m:P * m + QROWS[m]], by_batch[:, c, :, 0:T], start=c == 0, stop=c == EC - 1)
                for c in range(EC):
                    last = mm(ps[:, :, T:TOK], wkip[:, c, P * m:P * m + QROWS[m]], by_batch[:, c, :, T:TOK],
                              start=c == 0, stop=c == EC - 1)
                last.then_inc(pre_k, 1)
                if m == 0:
                    pe.wait_ge(wq_lo_made, 1)
                q_project(Batch(0), 0, m)
            pe.wait_ge(in_wv, DMA)
            for q in range(PAIRS):
                if q == 3:
                    pe.wait_ge(k_lo, 4)
                for c in range(EC):
                    last = mm(BANKS[1 + q][:, 0:C], ctxT[:, c, P * q:P * q + P], wv[:, c, :], start=c == 0, stop=c == EC - 1)
                last.then_inc(pre_v, 1)
            pe.wait_ge(ipn_made, 1)
            pe.wait_ge(k_lo, 8)
            for c in range(EC):
                last = tr(BANKS[5][:, 32 * c:32 * c + 32], ipn[:, P * c:P * c + P], ident[0:B * NIP, 0:B * NIP])
            last.then_inc(pre_ipn, 1)
            pe.wait_ge(in_wvip, DMA)
            pe.wait_ge(k_lo, 10)
            for m in range(QC):
                for c in range(EC):
                    last = mm(BANKS[0][0:QROWS[m], 32 * m:32 * m + 32].rearrange("p (b n) -> p b n", n=NIP),
                              wvip[:, c, P * m:P * m + QROWS[m]], by_batch[:, c, :, T:TOK], start=c == 0, stop=c == EC - 1)
            last.then_inc(pre_vip, 1)
            pe.wait_ge(ctxM_made, 2)
            pe.wait_ge(v_copied, 1)
            for q in range(PAIRS):
                for c in range(EC):
                    last = mm(BANKS[1][:, P * q:P * q + P], ctxT[:, c, P * q:P * q + P], ctxM[:, c, P * q:P * q + P],
                              start=c == 0, stop=c == EC - 1)
            last.then_inc(pre_g, 1)
            pe.wait_ge(vip_made, QC)
            pe.wait_ge(in_wo, 2 * DMA)
            pe.wait_ge(v_copied, PAIRS)
            for n in range(5):
                m, part = (n // 2, n % 2) if n < 4 else (2, 0)
                if n == 4:
                    pe.wait_ge(u_copied, 1)
                mm(BANKS[(2, 3, 4, 5, 2)[n]][:, 0:C], vip_bd[0:QROWS[m], m, P * part:P * part + P], wo[0:QROWS[m], m, :],
                   start=True, stop=True).then_inc(pre_u, 1)
            pe.wait_ge(g_copied, 2)
            scores(Batch(0), 0)
            scores(Batch(0), 1)
            pe.wait_ge(u_copied, 5)
            pe.wait_ge(zeros_made, 6)
            e_transposes(Batch(0), 0)
            scores(Batch(0), 2)
            e_transposes(Batch(0), 1)
            scores(Batch(0), 3)

            def slot(batch, u):
                if batch.has(UNITS, u + SLEAD, ALL_UNITS):
                    scores(batch, u + SLEAD)
                if batch.has(UNITS, u + TLEAD, ALL_UNITS):
                    e_transposes(batch, u + TLEAD)
                if batch.has(UNITS, u, ALL_UNITS):
                    table_products(batch, u)
                kind, n, h, t = misc_task(batch, u - 1)
                if kind == "o":
                    if batch.number == 0 and t == 0:
                        pe.wait_ge(u_placed, 3 * B * DMA)
                    out_project(batch, h, n, t, 1)
                kind, n, h, t = misc_task(batch, u)
                if kind == "x":
                    x_transposes(batch, h + 1, n)
                if kind == "q":
                    q_project(batch, h + 1, n)
                if kind == "at":
                    attn_transposes(batch, h, n, t)
                if kind == "o":
                    out_project(batch, h, n, t, 0)

            def body(batch):
                for u in range(UNITS):
                    slot(batch, u)

            def drain(batch):
                for u in range(3 * GROUPS - 2):
                    slot(batch, u)

            run_batches(pe, body, body, drain)


_INS = ["x", "ctx_2048", "fside_S_0", "L0_xattn_W_q", "L0_xattn_W_k", "L0_xattn_W_v",
        "L0_xattn_W_k_ip", "L0_xattn_W_v_ip", "L0_xattn_W_out", "L0_xattn_b_out"]


def kernel(**inputs):
    import numpy as _np
    import concourse.bacc as _bacc
    from concourse.bass_utils import run_bass_kernel_spmd as _run

    nc = _bacc.Bacc("TRN2", target_bir_lowering=False, num_devices=1)
    arrays, args = {}, []
    for name in _INS:
        a = _np.ascontiguousarray(inputs[name])
        arrays[f"in_{name}"] = a
        args.append(nc.dram_tensor(f"in_{name}", a.shape, mybir.dt.from_np(a.dtype), kind="ExternalInput").ap())
    out = nc.dram_tensor("out", inputs["x"].shape, F32, kind="ExternalOutput").ap()
    with nc.allow_non_contiguous_dma(reason="the spatial mask is 512 numbers, one column a tile"):
        xattn_kernel(nc, *args, out)
    r = _run(nc, [arrays], core_ids=[0])
    return r.results[0]["out"]
```

```python
import math
from contextlib import ExitStack

import concourse.bass as bass
from concourse import mybir

F32 = mybir.dt.float32
F32R = mybir.dt.float32r
ALU = mybir.AluOpType
ACT = mybir.ActivationFunctionType
AX_X = mybir.AxisListType.X

P = 128
HEADS = 20
NIP = 4
SEM_SCALE = 0.5
EPS = 1e-12
GROUP = 4
DMA = 16


class Batch:

    def __init__(self, number=None, step=None, place=0):
        self.number, self.step, self.place = number, step, place
        self.parity = (number if step is None else 1 + place) % 2

    def count(self, per_batch, extra):
        if self.step is None:
            return self.number * per_batch + extra
        return self.step * (2 * per_batch) + ((1 + self.place) * per_batch + extra)

    def has(self, per_batch, extra, end):
        return self.step is not None or 0 <= self.number * per_batch + extra < end

    def slot(self, per_batch, extra, ring):
        if self.step is None:
            return (self.number * per_batch + extra) % ring, (self.number * per_batch + extra) // ring
        at = (1 + self.place) * per_batch + extra
        return at % ring, self.step * (2 * per_batch // ring) + at // ring


def xattn_kernel(nc, x, ctx_tokens, ip_mask, w_q, w_k, w_v, w_k_ip, w_v_ip, w_out, b_out, out):
    B, S, C = x.shape
    _, TOK, E = ctx_tokens.shape
    T = TOK - NIP
    D = C // HEADS
    SCALE = D ** -0.5
    TILES = S // P
    HALVES = TILES // 2
    HALF = 2 * P
    GROUPS = HEADS // GROUP
    UNITS = TILES * GROUPS
    GROWS = GROUP * D
    EC = E // P
    QC = -(-C // P)
    QROWS = [min(P, C - P * m) for m in range(QC)]
    PAIRS = B // 2
    TABW = TOK + D + 1
    FINW = NIP + D + 1
    ALL_UNITS, ALL_TILES, ALL_HALVES = B * UNITS, B * TILES, B * HALVES
    XRING, YRING, SRING = 4, TILES, TILES
    ERING, TRING = 5, 4
    SLEAD, LEAD, TLEAD = 4, 3, 2
    HPC = P // D
    IPROWS = HEADS * NIP
    KM_STEPS, GV_STEPS = GROUPS, 6
    assert TOK * 2 == P and C == 2 * P + 64 and GROWS * 2 == P and B == 8 and TILES == 4

    es = ExitStack()
    with es:
        def sb(name, shape, dt=F32):
            return es.enter_context(nc.sbuf_tensor(name, shape, dt))

        def pb(name, shape):
            return es.enter_context(nc.psum_tensor(name, shape, F32))

        def sem(name):
            return es.enter_context(nc.semaphore(name))

        place_ctx = sb("place_ctx", [P, PAIRS * E])
        place_w = sb("place_w", [P, 4 * EC * C])
        place_ctxT = sb("place_ctxT", [P, 2 * EC * B * TOK])
        place_used = {}

        def again(place, *shape):
            start = place_used.get(place.name, 0)
            place_used[place.name] = start + math.prod(shape)
            names = "abc"[:len(shape)]
            return place[:, start:start + math.prod(shape)].rearrange(
                f"p ({' '.join(names)}) -> p {' '.join(names)}", **dict(zip(names, shape)))

        ctx_nat = place_ctx[:].rearrange("p (q e) -> p q e", q=PAIRS)
        ip_nat = sb("ip_nat", [B * NIP, E])
        wk, wv, wkip, wvip = (
            place_w[:, EC * C * n:EC * C * (n + 1)].rearrange("p (c n) -> p c n", c=EC) for n in range(4))
        wq_nat = sb("wq_nat", [P, QC, C])
        wq_hi = sb("wq_hi", [P, QC, C], F32R)
        wq_lo = sb("wq_lo", [P, QC, C], F32R)
        wo = sb("wo", [P, QC, C])
        wo_parts = sb("wo_parts", [P, 2, QC, C], F32R)
        bias_all = sb("bias_all", [P, C])
        mask_sb = sb("mask_sb", [P, TILES])
        x_nat = sb("x_nat", [P, XRING, 2, C])
        ident = sb("ident", [P, P])
        head_of_row = sb("head_of_row", [P, HPC])
        group_mask = sb("group_mask", [P, GROUP])
        neg_half = sb("neg_half", [P, HEADS])
        ctxT, ctxM = (
            place_ctxT[:, EC * B * TOK * n:EC * B * TOK * (n + 1)].rearrange("p (c t) -> p c t", c=EC) for n in range(2))
        ipn = sb("ipn", [B * NIP, E])
        ip_sq = sb("ip_sq", [B * NIP, E])
        ip_ss = sb("ip_ss", [B * NIP, 1])
        ip_ssc = sb("ip_ssc", [B * NIP, 1])
        ip_rn = sb("ip_rn", [B * NIP, 1])
        ktok = sb("ktok", [P, 2, GROUPS, B * TOK], F32R)
        g_sb = sb("g_sb", [P, PAIRS, TOK])
        v_sb = again(place_ctx, PAIRS, C)
        vip_bd = again(place_ctx, QC, B * HPC * NIP)
        u_sb = again(place_w, 5, C)
        u_nat = again(place_ctxT, B, C)
        u_all = sb("u_all", [P, B, 2, C], F32R)
        wv_hi, wv_lo, wk_hi, wk_lo = (
            u_all[:].rearrange("p b s c -> p (b s c)")[:, EC * C * n:EC * C * (n + 1)].rearrange("p (c n) -> p c n", c=EC)
            for n in range(4))
        km = sb("km", [P, 2, GROUPS, 2, GROUP * TOK], F32R)
        ctx_hi = km[:, 1].rearrange("p g s t -> p (g s t)")[:, 0:EC * B * TOK].rearrange("p (c t) -> p c t", c=EC)
        ctx_lo = sb("ctx_lo", [P, EC, B * TOK], F32R)
        tab = sb("tab", [P, 2, HEADS, TABW])
        xh = sb("xh", [P, QC, HALF], F32R)
        xl = sb("xl", [P, QC - 1, HALF], F32R)
        qs = sb("qs", [P, 2, GROUPS, HALF], F32R)
        negmax = sb("negmax", [P, ERING, GROUP])
        e_sb = sb("e_sb", [P, ERING, GROUP * TOK])
        eT = again(place_w, TRING, 2 * P)
        junk = again(place_ctxT, 2, GROUP, TOK)
        quad = sb("quad", [P, 2, HEADS])
        sip = sb("sip", [P, SRING, HEADS, NIP])
        fin = again(place_ctxT, 2, HEADS, FINW)
        guard = sb("guard", [P, 2, HEADS])
        quadc = sb("quadc", [P, 2, HEADS])
        rsum = sb("rsum", [P, 2, HEADS])
        lnq = sb("lnq", [P, 2, HEADS])
        rnorm = sb("rnorm", [P, 2, HEADS])
        semn = sb("semn", [P, 2, HEADS, NIP])
        fused = sb("fused", [P, 2, HEADS, NIP])
        ipmax = sb("ipmax", [P, 2, HEADS])
        ipd = sb("ipd", [P, 2, HEADS, NIP])
        ipe = sb("ipe", [P, 2, HEADS, NIP])
        ipsum = sb("ipsum", [P, 2, HEADS])
        iprec = sb("iprec", [P, 2, HEADS])
        ipw = sb("ipw", [P, 2, HEADS])
        pip = sb("pip", [P, 2, HEADS, NIP])
        attn = again(place_w, 2, C)
        attnT = sb("attnT", [P, 4 * P], F32R)
        attnT_low = sb("attnT_low", [P, 3 * P], F32R)
        y_sb = again(place_w, YRING, C)

        sc_ps = pb("sc_ps", [P, 2, 512])
        et_ps = pb("et_ps", [P, 2, 512])
        gv_ps = pb("gv_ps", [P, 2, 512])
        mi_ps = pb("mi_ps", [P, 2, 512])
        BANKS = [sc_ps[:, 0, :], sc_ps[:, 1, :], et_ps[:, 0, :], et_ps[:, 1, :], gv_ps[:, 0, :], gv_ps[:, 1, :]]

        in_ctx, in_wk, in_wq, in_wv = [sem(f"in_ctx{q}") for q in range(PAIRS)], sem("in_wk"), sem("in_wq"), sem("in_wv")
        in_wkip, in_wvip, in_wo, in_ip = sem("in_wkip"), sem("in_wvip"), sem("in_wo"), sem("in_ip")
        in_bias, in_mask = sem("in_bias"), sem("in_mask")
        in_x = [sem(f"in_x{n}") for n in range(XRING)]
        y_stored = [sem(f"y_stored{n}") for n in range(YRING)]
        consts_step, ident_made, consts_made, zeros_made = (
            sem("consts_step"), sem("ident_made"), sem("consts_made"), sem("zeros_made"))
        pre_ctxT, pre_k, pre_v, pre_ipn, pre_g, pre_vip, pre_u = (
            sem(f"pre_{n}") for n in ("ctxT", "k", "v", "ipn", "g", "vip", "u"))
        ctxT_act, ctxT_dve, ctxM_text, ctxM_made = (
            sem("ctxT_act"), sem("ctxT_dve"), sem("ctxM_text"), sem("ctxM_made"))
        ip_step, ip_rn_made, ipn_made = sem("ip_step"), sem("ip_rn_made"), sem("ipn_made")
        k_hi, k_lo, v_copied, g_copied, vip_made = (
            sem("k_hi"), sem("k_lo"), sem("v_copied"), sem("g_copied"), sem("vip_made"))
        wo_hi_made, wo_lo_made, u_lo_made = sem("wo_hi_made"), sem("wo_lo_made"), sem("u_lo_made")
        u_hi_made = sem("u_hi_made")
        ctx_hi_made, ctx_lo_made = sem("ctx_hi_made"), sem("ctx_lo_made")
        wv_hi_made, wv_lo_made, wk_hi_made, wk_lo_made = sem("wv_hi_made"), sem("wv_lo_made"), sem("wk_hi_made"), sem("wk_lo_made")
        u_copied, u_placed, wq_hi_made, wq_lo_made = (
            sem("u_copied"), sem("u_placed"), sem("wq_hi_made"), sem("wq_lo_made"))
        xT_done, xT_hi, xT_lo = sem("xT_done"), sem("xT_hi"), sem("xT_lo")
        q_done, q_hi, q_lo = sem("q_done"), sem("q_hi"), sem("q_lo")
        xb_made = sem("xb_made")
        pool_turn = sem("pool_turn")
        km_made, tab_made = sem("km_made"), sem("tab_made")
        scores_done, max_done, exp_done = sem("scores_done"), sem("max_done"), sem("exp_done")
        eT_done, eT_copied = sem("eT_done"), sem("eT_copied")
        gv_done, quad_done, fin_copied = sem("gv_done"), sem("quad_done"), sem("fin_copied")
        guard_made, quadc_made, rsum_made = sem("guard_made"), sem("quadc_made"), sem("rsum_made")
        lnq_made = sem("lnq_made")
        rnorm_made, semn_made, fused_made = sem("rnorm_made"), sem("semn_made"), sem("fused_made")
        attn_made, ipmax_made, ipd_made, ipe_made = (
            sem("attn_made"), sem("ipmax_made"), sem("ipd_made"), sem("ipe_made"))
        ipsum_made, iprec_made, ipw_made, pip_made = (
            sem("ipsum_made"), sem("iprec_made"), sem("ipw_made"), sem("pip_made"))
        attnT_done, attnT_hi, attnT_lo, out_done, y_made = (
            sem("attnT_done"), sem("attnT_hi"), sem("attnT_lo"), sem("out_done"), sem("y_made"))
        last_done, last_hi, last_lo = sem("last_done"), sem("last_hi"), sem("last_lo")
        LAST_ATTN, LAST_IP, LAST_OUT = BANKS[0], BANKS[1][:, 0:P], BANKS[2][:, 0:C]
        last_attnT, last_attnT_low = xh[:].rearrange("p c t -> p (c t)"), xl[:].rearrange("p c t -> p (c t)")

        out_t = out.rearrange("b (t p) c -> (b t) p c", p=P)

        def x_half(half):
            return x.rearrange("b (h t p) c -> (b h) p t c", p=P, t=2)[half]

        MISC_SLOTS = {0: ("x", 0), 1: ("o", 1), 2: ("x", 1), 3: ("q", 0), 4: ("at", 0),
                      5: ("q", 1), 6: ("o", 0), 8: ("q", 2), 9: ("at", 1)}
        MISC_ORDER = list(MISC_SLOTS.values())
        TASK_TILE = {("o", 1): -3, ("at", 0): -2, ("o", 0): -2, ("at", 1): -1}
        FIRST_BANK = {("x", 0): 0, ("x", 1): 1, ("q", 0): 0, ("q", 1): 1, ("q", 2): 0}

        def misc_bank(batch, half, kind, n):
            if batch.number == 0 and half == -1:
                return FIRST_BANK[kind, n]
            return (9 * half + MISC_ORDER.index((kind, n))) % 2

        def bank_released(batch, half, kind, n):
            if batch.number == 0 and half == -1:
                return (q_lo, 1) if (kind, n) == ("q", 2) else None
            at = 9 * half + MISC_ORDER.index((kind, n)) - 2
            while True:
                hh, (k, m) = at // 9, MISC_ORDER[at % 9]
                if k in "xq":
                    if batch.has(HALVES, hh + 1, ALL_HALVES):
                        if k == "x":
                            return xT_lo, batch.count(2 * HALVES, 2 * (hh + 1) + m + 1)
                        return q_lo, batch.count(3 * HALVES, 3 * (hh + 1) + m + 1)
                else:
                    t = 2 * hh + TASK_TILE[k, m]
                    if batch.has(TILES, t, ALL_TILES):
                        return (attnT_lo if k == "at" else y_made), batch.count(TILES, t + 1)
                at -= 2
                if batch.step is None and 2 * batch.number + at // 9 < -1:
                    return None

        def misc_task(batch, at):
            h, hu = divmod(at, UNITS // HALVES)
            kind, n = MISC_SLOTS.get(hu, ("", 0))
            if kind in ("x", "q") and batch.has(HALVES, h + 1, ALL_HALVES):
                return kind, n, h, None
            if batch.number == B and 2 * h + TASK_TILE.get((kind, n), 0) == -1:
                return "", 0, 0, None
            if kind in ("at", "o") and batch.has(TILES, 2 * h + TASK_TILE[kind, n], ALL_TILES):
                return kind, n, h, 2 * h + TASK_TILE[kind, n]
            return "", 0, 0, None

        K_BANKS, U_BANKS = (5, 4, 3), (3, 4, 5, 3, 4)
        U_SLOT = 10
        LOOP_STEPS = (B - 2) // 2

        def run_batches(eng, first, body, last):
            first(Batch(0))
            with eng.Fori(0, LOOP_STEPS) as step:
                for place in range(2):
                    body(Batch(step=step, place=place))
            body(Batch(B - 1))
            last(Batch(B))

        block = es.enter_context(nc.Block())

        @block.sync
        def _(sp):
            for q in range(PAIRS):
                sp.dma_start(ctx_nat[:, q, :], ctx_tokens.rearrange("(q b) t e -> q (b t) e", b=2)[q]).then_inc(in_ctx[q], DMA)
                if q == 0:
                    sp.dma_start(ip_nat[:], ctx_tokens[:, T:TOK, :]).then_inc(in_ip, DMA)
            sp.dma_start(x_nat[:, 0], x_half(0)).then_inc(in_x[0], DMA)
            sp.dma_start(wv, w_v.rearrange("(c p) n -> p c n", p=P)).then_inc(in_wv, DMA)
            sp.dma_start(wk, w_k.rearrange("(c p) n -> p c n", p=P)).then_inc(in_wk, DMA)
            sp.dma_start(wkip, w_k_ip.rearrange("(c p) n -> p c n", p=P)).then_inc(in_wkip, DMA)

            def load_square(nat, w, loaded):
                sp.dma_start(nat[:, 0:QC - 1], w[0:2 * P, :].rearrange("(c p) n -> p c n", p=P)).then_inc(loaded, DMA)
                for row in (0, 64):
                    sp.dma_start(nat[row:row + 64, QC - 1], w[2 * P:C, :]).then_inc(loaded, DMA)

            load_square(wq_nat, w_q, in_wq)
            sp.dma_start(wvip, w_v_ip.rearrange("(c p) n -> p c n", p=P)).then_inc(in_wvip, DMA)
            load_square(wo, w_out, in_wo)
            sp.dma_start(bias_all[:], b_out.rearrange("(a c) -> a c", a=1).to_broadcast([P, C])).then_inc(in_bias, DMA)
            sp.dma_start(mask_sb[:], ip_mask.rearrange("(t p) -> p t", p=P)).then_inc(in_mask, DMA)
            for half in range(1, XRING):
                sp.dma_start(x_nat[:, half], x_half(half)).then_inc(in_x[half], DMA)
            sp.wait_ge(u_copied, 5)
            for b in range(B):
                for m in range(2):
                    r, blk = 32 * (b % 4), 2 * m + b // 4
                    sp.dma_start(u_nat[32 * m:32 * m + 32, b], u_sb[r:r + 32, blk]).then_inc(u_placed, DMA)
                sp.dma_start(u_nat[64:80, b], u_sb[16 * b:16 * b + 16, 4]).then_inc(u_placed, DMA)

            def store(batch, s):
                sp.wait_ge(y_made, batch.count(TILES, s + 1))
                sp.dma_start(out_t[batch.count(TILES, s)], y_sb[:, s]).then_inc(y_stored[s], DMA)

            def stores_and_loads(batch, number):
                for h in range(HALVES):
                    store(batch, 2 * h)
                    store(batch, 2 * h + 1)
                    if number is None or number < B - 2:
                        slot, _ = batch.slot(HALVES, h, XRING)
                        sp.dma_start(x_nat[:, slot], x_half(batch.count(HALVES, h + XRING))).then_inc(in_x[slot], DMA)

            stores_and_loads(Batch(0), 0)
            with sp.Fori(0, LOOP_STEPS - 1) as step:
                for place in range(2):
                    stores_and_loads(Batch(step=step, place=place), None)
            for number in range(B - 3, B):
                stores_and_loads(Batch(number), number)
            for s in range(YRING):
                sp.wait_ge(y_stored[s], DMA * (B + 1))

        @block.gpsimd
        def _(pool):
            g = nc.gpsimd
            g.memset(ident[:], 0.0).then_inc(consts_step, 1)
            pool.wait_ge(consts_step, 1)
            g.affine_select(out=ident[:], in_=ident[:], compare_op=ALU.not_equal, fill=1.0, base=0,
                            pattern=[[-1, P]], channel_multiplier=1).then_inc(ident_made, 1)
            g.memset(head_of_row[:], 1.0).then_inc(consts_step, 1)
            pool.wait_ge(consts_step, 2)
            g.affine_select(out=head_of_row[:], in_=head_of_row[:], compare_op=ALU.is_ge, fill=0.0, base=0,
                            pattern=[[-D, HPC]], channel_multiplier=1).then_inc(consts_step, 1)
            pool.wait_ge(consts_step, 3)
            g.affine_select(out=head_of_row[:], in_=head_of_row[:], compare_op=ALU.is_ge, fill=0.0, base=D - 1,
                            pattern=[[D, HPC]], channel_multiplier=-1).then_inc(consts_step, 1)
            pool.wait_ge(consts_step, 4)
            g.tensor_copy(group_mask[0:64], head_of_row[0:64, 0:GROUP]).then_inc(consts_made, 1)
            pool.wait_ge(consts_made, 1)
            g.tensor_copy(group_mask[64:P], head_of_row[64:P, GROUP:HPC]).then_inc(consts_made, 1)
            pool.wait_ge(consts_made, 2)
            g.memset(neg_half[:], -0.5).then_inc(consts_made, 1)
            g.memset(e_sb[:].rearrange("p r (h t) -> p (r h) t", t=TOK)[:, :, T:TOK], 0.0).then_inc(zeros_made, 1)
            pool.wait_ge(consts_made, 3)
            pool.wait_ge(ip_step, 2)
            g.tensor_tensor(ip_rn[:], ip_ssc[:], neg_half[0:B * NIP, 0:1], ALU.pow).then_inc(ip_rn_made, 1)
            pool.wait_ge(zeros_made, 2)
            pool.wait_ge(ip_rn_made, 1)
            for par in range(2):
                for r in range(2):
                    g.memset(tab[64 * r:64 * r + T, par, r::2, TABW - 1:TABW], 1.0).then_inc(zeros_made, 1)
                    pool.wait_ge(zeros_made, 3 + 2 * par + r)

            def km_step(batch, c):
                cols = batch.count(TOK, 0)
                g.tensor_tensor(
                    km[:, batch.parity, c].rearrange("p s (j t) -> p s j t", t=TOK),
                    ktok[:, :, c, bass.ds(cols, TOK)].unsqueeze(2).to_broadcast([P, 2, GROUP, TOK]),
                    group_mask[:].unsqueeze(1).unsqueeze(3).to_broadcast([P, 2, GROUP, TOK]),
                    ALU.mult).then_inc(km_made, 1)

            def tab_step(batch, n):
                r = n % 2
                _, pair = batch.slot(1, 0, 2)
                src = 64 * batch.parity
                rows = slice(64 * r, 64 * r + T)
                if n < 4:
                    h0 = 10 * (n // 2) + r
                    g.tensor_copy(tab[rows, batch.parity, h0:h0 + 9:2, 0:TOK],
                                  g_sb[src:src + T, pair, :].unsqueeze(1).to_broadcast([T, 5, TOK])
                                  if isinstance(pair, int) else
                                  g_sb[src:src + T, bass.ds(pair, 1), :].to_broadcast([T, 5, TOK])).then_inc(tab_made, 1)
                else:
                    v = v_sb[src:src + T, bass.ds(pair, 1), :].rearrange("p a (h d) -> p (a h) d", d=D)
                    g.tensor_copy(tab[rows, batch.parity, r::2, TOK:TOK + D], v[:, r::2, :]).then_inc(tab_made, 1)
                pool.wait_ge(tab_made, batch.count(GV_STEPS, n + 1))
                pool.sem_inc(pool_turn, 1)

            def add_bias(batch, half):
                slot, _ = batch.slot(HALVES, half, XRING)
                pool.wait_ge(xT_done, batch.count(2 * HALVES, 2 * half + 2))
                g.tensor_tensor(x_nat[:, slot], x_nat[:, slot],
                                bias_all[:].unsqueeze(1).to_broadcast([P, 2, C]), ALU.add).then_inc(xb_made, 1)

            pool.wait_ge(zeros_made, 6)
            pool.wait_ge(g_copied, 2)
            for n in range(GV_STEPS):
                if n == 4:
                    pool.wait_ge(v_copied, 1)
                tab_step(Batch(0), n)
            for c in range(GROUPS):
                pool.wait_ge(k_hi, 2 * c + 2)
                pool.wait_ge(k_lo, 2 * c + 2)
                km_step(Batch(0), c)
            pool.wait_ge(in_bias, DMA)
            pool.wait_ge(in_mask, DMA)
            add_bias(Batch(0), 0)

            def nxt(batch):
                return (Batch(batch.number + 1) if batch.step is None else
                        Batch(step=batch.step, place=batch.place + 1))

            def builds(batch, s, part):
                if not batch.has(1, 1, B):
                    return
                to = nxt(batch)
                k = 2 * s + part
                if k == 0 and batch.number == 0:
                    pool.wait_ge(v_copied, PAIRS)
                if k == 0 and batch.has(1, -1, B):
                    pool.wait_ge(scores_done, batch.count(UNITS, 0))
                    pool.wait_ge(gv_done, batch.count(UNITS, 0))
                for c in ((0,), (1,), (2,), (3,), (4,), (), (), ())[k]:
                    km_step(to, c)
                if k in (5, 7):
                    pool.wait_ge(fused_made, batch.count(TILES, s))
                    pool.sem_inc(pool_turn, 1)
                for n in ((), (), (), (), (), (0, 1), (2, 3), (4, 5))[k]:
                    tab_step(to, n)

            def tile(batch, s):
                builds(batch, s, 0)
                if batch.has(TILES, s - 1, ALL_TILES):
                    n, par = batch.count(TILES, s), (s - 1) % 2
                    pool.wait_ge(rsum_made, n)
                    g.tensor_tensor(attn[:, par].rearrange("p (h d) -> p h d", d=D), fin[:, par, :, NIP:NIP + D],
                                    rsum[:, par].unsqueeze(2).to_broadcast([P, HEADS, D]), ALU.mult).then_inc(attn_made, 1)
                if batch.has(TILES, s - 2, ALL_TILES):
                    par2, st = s % 2, (s - 2) % TILES
                    pool.wait_ge(iprec_made, batch.count(TILES, s - 1))
                    pool.sem_inc(pool_turn, 1)
                    g.tensor_scalar(ipw[:, par2], iprec[:, par2], mask_sb[:, st:st + 1], None, ALU.mult).then_inc(ipw_made, 1)
                    pool.wait_ge(ipw_made, batch.count(TILES, s - 1))
                    g.tensor_tensor(pip[:, par2], ipe[:, par2],
                                    ipw[:, par2].unsqueeze(2).to_broadcast([P, HEADS, NIP]), ALU.mult).then_inc(pip_made, 1)
                if batch.has(TILES, s - 1, ALL_TILES):
                    pool.wait_ge(rnorm_made, n)
                    g.tensor_tensor(semn[:, par], fin[:, par, :, 0:NIP],
                                    rnorm[:, par].unsqueeze(2).to_broadcast([P, HEADS, NIP]), ALU.mult).then_inc(semn_made, 1)
                    pool.wait_ge(semn_made, n)
                    g.tensor_tensor(fused[:, par], semn[:, par], sip[:, (s - 1) % SRING], ALU.add).then_inc(fused_made, 1)
                builds(batch, s, 1)
                if s % 2 == 1 and batch.has(HALVES, s // 2 + 1, ALL_HALVES):
                    add_bias(batch, s // 2 + 1)

            def body(batch):
                for s in range(TILES):
                    tile(batch, s)

            def drain(batch):
                for s in range(2):
                    tile(batch, s)

            run_batches(pool, body, body, drain)

        @block.scalar
        def _(act):
            nc.scalar.preload_act_table_set("natural_log_exp_and_others")
            def x_hi(batch, half, n):
                act.wait_ge(xT_done, batch.count(2 * HALVES, 2 * half + n + 1))
                ps = mi_ps[:, misc_bank(batch, half - 1, "x", n), :]
                if n == 0:
                    nc.scalar.copy(xh[:, 0:2, :], ps.rearrange("p (c t) -> p c t", c=2)).then_inc(xT_hi, 1)
                else:
                    nc.scalar.copy(xh[0:64, 2, :], ps[64:P, 0:HALF]).then_inc(xT_hi, 1)

            def q_high(batch, half, m):
                act.wait_ge(q_done, batch.count(3 * HALVES, 3 * half + m + 1))
                ps = mi_ps[:, misc_bank(batch, half - 1, "q", m), :]
                for a in range(QROWS[m] // 64):
                    last = nc.scalar.copy(qs[0:64, half % 2, 2 * m + a, :], ps[64 * a:64 * a + 64, 0:HALF])
                last.then_inc(q_hi, 1)

            def exps(batch, u):
                slot, bank = u % ERING, u % 2
                act.wait_ge(max_done, batch.count(UNITS, u + 1))
                for j in range(GROUP):
                    last = nc.scalar.activation(e_sb[:, slot, TOK * j:TOK * j + T], sc_ps[:, bank, TOK * j:TOK * j + T],
                                                ACT.Exp, bias=negmax[:, slot, j:j + 1])
                last.then_inc(exp_done, 1)

            def copy_fin(batch, u):
                s, c = divmod(u, GROUPS)
                act.wait_ge(quad_done, batch.count(UNITS, u + 1))
                ps = gv_ps[:, u % 2, 0:GROUP * TABW].rearrange("p (h w) -> p h w", w=TABW)
                nc.scalar.copy(fin[:, s % 2, GROUP * c:GROUP * c + GROUP, :], ps[:, :, TOK - NIP:TABW]).then_inc(fin_copied, 1)

            def copy_eT(batch, u):
                act.wait_ge(eT_done, batch.count(UNITS, u + 1))
                nc.scalar.copy(eT[:, u % TRING, :], et_ps[:, u % 2, 0:2 * P]).then_inc(eT_copied, 1)

            for q in range(PAIRS):
                if q % 2 == 0:
                    act.wait_ge(pre_ctxT, q + 1)
                    nc.scalar.copy(ctxT[:, :, P * q:P * q + P],
                                   BANKS[q].rearrange("p (c t) -> p c t", c=EC)).then_inc(ctxT_act, 1)
                else:
                    act.wait_ge(ctxT_dve, q // 2 + 1)
                nc.scalar.copy(ctxM[:, :, P * q:P * q + P].rearrange("p c (b t) -> p c b t", t=TOK)[:, :, :, 0:T],
                               BANKS[q].rearrange("p (c b t) -> p c b t", b=2, t=TOK)[:, :, :, 0:T]).then_inc(ctxM_text, 1)
            x_hi(Batch(0), 0, 0)
            x_hi(Batch(0), 0, 1)
            act.wait_ge(ctxT_act, 2)
            act.wait_ge(ctxT_dve, 2)
            nc.scalar.copy(ctx_hi, ctxT).then_inc(ctx_hi_made, 1)
            act.wait_ge(in_wv, DMA)
            nc.scalar.copy(wv_hi, wv).then_inc(wv_hi_made, 1)
            act.wait_ge(in_wk, DMA)
            nc.scalar.copy(wk_hi, wk).then_inc(wk_hi_made, 1)
            act.wait_ge(in_wq, 3 * DMA)
            nc.scalar.copy(wq_hi[:], wq_nat[:]).then_inc(wq_hi_made, 1)
            act.wait_ge(in_wo, 3 * DMA)
            nc.scalar.copy(wo_parts[:, 0], wo[:]).then_inc(wo_hi_made, 1)
            for q in range(PAIRS - 1):
                act.wait_ge(pre_v, q + 1)
                nc.scalar.copy(v_sb[:, q, :], BANKS[q][:, 0:C]).then_inc(v_copied, 1)
            for m in range(QC):
                act.wait_ge(pre_k, m + 1)
                for a in range(QROWS[m] // 64):
                    for half in range(2):
                        nc.scalar.activation(ktok[64 * half:64 * half + 64, 0, 2 * m + a, :],
                                             BANKS[K_BANKS[m]][64 * a:64 * a + 64, :], ACT.Copy, scale=SCALE).then_inc(k_hi, 1)
                if m > 0:
                    q_high(Batch(0), 0, m - 1)
            q_high(Batch(0), 0, 2)
            exps(Batch(0), 0)
            exps(Batch(0), 1)
            act.wait_ge(pre_v, PAIRS)
            nc.scalar.copy(v_sb[:, PAIRS - 1, :], mi_ps[:, 1, 0:C]).then_inc(v_copied, 1)
            copy_eT(Batch(0), 0)
            for n in range(5):
                act.wait_ge(pre_u, n + 1)
                nc.scalar.copy(u_sb[:, n], BANKS[U_BANKS[n]][:, 0:C]).then_inc(u_copied, 1)
            exps(Batch(0), 2)
            copy_eT(Batch(0), 1)

            def slot(batch, u):
                s, j = divmod(u, GROUPS)
                before, par, n = batch.has(TILES, s - 1, ALL_TILES), (s - 1) % 2, batch.count(TILES, s)
                if batch.has(UNITS, u - 2, ALL_UNITS):
                    copy_fin(batch, u - 2)
                kind, m, h, t = misc_task(batch, u - 1)
                if kind == "x":
                    x_hi(batch, h + 1, m)
                if kind == "q":
                    q_high(batch, h + 1, m)
                if kind == "at":
                    act.wait_ge(attnT_done, batch.count(TILES, t + 1))
                    ps = mi_ps[:, misc_bank(batch, h, "at", m), :]
                    nc.scalar.copy(attnT[:, 0:2 * P], ps[:, 0:2 * P])
                    nc.scalar.copy(attnT[0:64, 2 * P:3 * P], ps[0:64, 2 * P:3 * P])
                    nc.scalar.copy(attnT[0:IPROWS, 3 * P:4 * P], ps[0:IPROWS, 3 * P:4 * P]).then_inc(attnT_hi, 1)
                if j == 3 and before:
                    act.wait_ge(quadc_made, n)
                    nc.scalar.activation(lnq[:, par], quadc[:, par], ACT.Ln).then_inc(lnq_made, 1)
                if batch.has(UNITS, u + LEAD, ALL_UNITS):
                    exps(batch, u + LEAD)
                if j == 3 and before:
                    act.wait_ge(lnq_made, n)
                    nc.scalar.activation(rnorm[:, par], lnq[:, par], ACT.Exp, scale=-0.5).then_inc(rnorm_made, 1)
                if batch.has(UNITS, u + TLEAD, ALL_UNITS):
                    copy_eT(batch, u + TLEAD)
                if j == 0 and batch.has(TILES, s - 2, ALL_TILES):
                    act.wait_ge(ipd_made, batch.count(TILES, s - 1))
                    nc.scalar.activation(ipe[:, s % 2], ipd[:, s % 2], ACT.Exp).then_inc(ipe_made, 1)
                if batch.number == 0 and 0 <= u - U_SLOT < B:
                    if u == U_SLOT:
                        act.wait_ge(u_placed, 3 * B * DMA)
                    nc.scalar.copy(u_all[0:IPROWS, u - U_SLOT, 0], u_nat[0:IPROWS, u - U_SLOT]).then_inc(u_hi_made, 1)

            def body(batch):
                for u in range(UNITS):
                    slot(batch, u)

            def drain(batch):
                for u in range(GROUPS + 1):
                    slot(batch, u)
                act.wait_ge(last_done, 1)
                nc.scalar.copy(last_attnT[:, 0:2 * P], LAST_ATTN[:, 0:2 * P])
                nc.scalar.copy(last_attnT[0:64, 2 * P:3 * P], LAST_ATTN[0:64, 2 * P:3 * P]).then_inc(last_hi, 1)
                act.wait_ge(last_done, 2)
                nc.scalar.copy(last_attnT[0:IPROWS, 3 * P:4 * P], LAST_IP[0:IPROWS]).then_inc(last_hi, 1)

            run_batches(act, body, body, drain)

        @block.vector
        def _(dve):
            v = nc.vector
            v.memset(tab[:], 0.0).then_inc(zeros_made, 1)
            for place in range(YRING):
                dve.sem_inc(y_stored[place], DMA)

            def x_low(batch, half, n):
                dve.wait_ge(xT_hi, batch.count(2 * HALVES, 2 * half + n + 1))
                ps = mi_ps[:, misc_bank(batch, half - 1, "x", n), :]
                if n == 0:
                    v.tensor_tensor(xl[:], ps.rearrange("p (c t) -> p c t", c=2), xh[:, 0:2, :].bitcast(F32),
                                    ALU.subtract).then_inc(xT_lo, 1)
                else:
                    v.tensor_tensor(xh[64:P, 2, :], ps[64:P, 0:HALF], xh[0:64, 2, :].bitcast(F32),
                                    ALU.subtract).then_inc(xT_lo, 1)

            def q_low(batch, half, m):
                dve.wait_ge(q_hi, batch.count(3 * HALVES, 3 * half + m + 1))
                ps = mi_ps[:, misc_bank(batch, half - 1, "q", m), :]
                for a in range(QROWS[m] // 64):
                    c = 2 * m + a
                    last = v.tensor_tensor(qs[64:P, half % 2, c, :], ps[64 * a:64 * a + 64, 0:HALF],
                                           qs[0:64, half % 2, c, :].bitcast(F32), ALU.subtract)
                last.then_inc(q_lo, 1)

            def maxima(batch, u):
                s, c = divmod(u % UNITS, GROUPS)
                dve.wait_ge(scores_done, batch.count(UNITS, u + 1))
                ps = sc_ps[:, u % 2, 0:GROUP * TOK].rearrange("p (h t) -> p h t", t=TOK)
                v.tensor_copy(sip[:, s % SRING, GROUP * c:GROUP * c + GROUP, :], ps[:, :, T:TOK])
                v.tensor_reduce(negmax[:, u % ERING, :], ps[:, :, 0:T], AX_X, ALU.max, negate=True).then_inc(max_done, 1)

            def quadratic(batch, u):
                s, c = divmod(u, GROUPS)
                dve.wait_ge(gv_done, batch.count(UNITS, u + 1))
                for j in range(GROUP):
                    h = GROUP * c + j
                    last = v.tensor_tensor_reduce(
                        out=junk[:, u % 2, j, 0:T], in0=gv_ps[:, u % 2, TABW * j:TABW * j + T],
                        in1=e_sb[:, u % ERING, TOK * j:TOK * j + T], scale=1.0, scalar=0.0,
                        op0=ALU.mult, op1=ALU.add, accum_out=quad[:, s % 2, h:h + 1])
                last.then_inc(quad_done, 1)

            dve.wait_ge(in_ip, DMA)
            v.tensor_tensor_reduce(out=ip_sq[:], in0=ip_nat[:], in1=ip_nat[:], scale=1.0, scalar=0.0,
                                   op0=ALU.mult, op1=ALU.add, accum_out=ip_ss[:]).then_inc(ip_step, 1)
            dve.wait_ge(ip_step, 1)
            v.tensor_scalar(ip_ssc[:], ip_ss[:], EPS * EPS, None, ALU.max).then_inc(ip_step, 1)
            for q in (1, 3):
                dve.wait_ge(pre_ctxT, q + 1)
                v.tensor_copy(ctxT[:, :, P * q:P * q + P], BANKS[q].rearrange("p (c t) -> p c t", c=EC)).then_inc(ctxT_dve, 1)
                if q == 1:
                    dve.wait_ge(ip_rn_made, 1)
                    v.tensor_scalar(ipn[:], ip_nat[:], ip_rn[:], SEM_SCALE, ALU.mult, ALU.mult).then_inc(ipn_made, 1)
            dve.wait_ge(pre_ipn, 1)
            v.tensor_copy(ctxM.rearrange("p c (b t) -> p (c b) t", t=TOK)[:, :, T:TOK],
                          BANKS[5][:, 0:EC * B * NIP].rearrange("p (c n) -> p c n", n=NIP)).then_inc(ctxM_made, 1)
            x_low(Batch(0), 0, 0)
            x_low(Batch(0), 0, 1)
            dve.wait_ge(ctx_hi_made, 1)
            v.tensor_tensor(ctx_lo[:], ctxT, ctx_hi.bitcast(F32), ALU.subtract).then_inc(ctx_lo_made, 1)
            dve.wait_ge(wv_hi_made, 1)
            v.tensor_tensor(wv_lo, wv, wv_hi.bitcast(F32), ALU.subtract).then_inc(wv_lo_made, 1)
            dve.wait_ge(wk_hi_made, 1)
            v.tensor_tensor(wk_lo, wk, wk_hi.bitcast(F32), ALU.subtract).then_inc(wk_lo_made, 1)
            dve.wait_ge(wq_hi_made, 1)
            v.tensor_tensor(wq_lo[:], wq_nat[:], wq_hi[:].bitcast(F32), ALU.subtract).then_inc(wq_lo_made, 1)
            dve.wait_ge(pre_g, 1)
            for r in range(2):
                v.tensor_copy(g_sb[64 * r:64 * r + 64],
                              BANKS[4][64 * r:64 * r + 64, :].rearrange("p (q t) -> p q t", q=PAIRS)[:, :, 64 * r:64 * r + 64]
                              ).then_inc(g_copied, 1)
            dve.wait_ge(wo_hi_made, 1)
            v.tensor_tensor(wo_parts[:, 1], wo[:], wo_parts[:, 0].bitcast(F32), ALU.subtract).then_inc(wo_lo_made, 1)
            for m in range(QC):
                for a in range(QROWS[m] // 64):
                    for half in range(2):
                        c = 2 * m + a
                        dve.wait_ge(k_hi, 2 * c + 2)
                        v.scalar_tensor_tensor(out=ktok[64 * half:64 * half + 64, 1, c, :],
                                               in0=BANKS[K_BANKS[m]][64 * a:64 * a + 64, :], scalar=SCALE,
                                               in1=ktok[64 * half:64 * half + 64, 0, c, :].bitcast(F32),
                                               op0=ALU.mult, op1=ALU.subtract).then_inc(k_lo, 1)
                if m == 1:
                    q_low(Batch(0), 0, 0)
            maxima(Batch(0), 0)
            q_low(Batch(0), 0, 1)
            maxima(Batch(0), 1)
            q_low(Batch(0), 0, 2)
            dve.wait_ge(pre_vip, 1)
            for m in range(QC):
                hp = QROWS[m] // D
                rows = QROWS[m]
                v.tensor_tensor(
                    vip_bd[0:rows, m, 0:B * hp * NIP].rearrange("p (b h n) -> p b h n", h=hp, n=NIP),
                    BANKS[5][0:rows, 32 * m:32 * m + 32].rearrange("p (b n) -> p b n", n=NIP).unsqueeze(2)
                    .to_broadcast([rows, B, hp, NIP]),
                    head_of_row[0:rows, 0:hp].unsqueeze(1).unsqueeze(3).to_broadcast([rows, B, hp, NIP]),
                    ALU.mult).then_inc(vip_made, 1)
            maxima(Batch(0), 2)

            def attnT_lows(batch, bank, t):
                dve.wait_ge(attnT_hi, batch.count(TILES, t + 1))
                ps = mi_ps[:, bank, :]
                v.tensor_tensor(attnT_low[:, 0:2 * P], ps[:, 0:2 * P], attnT[:, 0:2 * P].bitcast(F32), ALU.subtract)
                v.tensor_tensor(attnT[64:P, 2 * P:3 * P], ps[0:64, 2 * P:3 * P], attnT[0:64, 2 * P:3 * P].bitcast(F32),
                                ALU.subtract)
                v.tensor_tensor(attnT_low[0:IPROWS, 2 * P:3 * P], ps[0:IPROWS, 3 * P:4 * P],
                                attnT[0:IPROWS, 3 * P:4 * P].bitcast(F32), ALU.subtract).then_inc(attnT_lo, 1)

            def add_residual(batch, bank, t):
                slot, _ = batch.slot(HALVES, t // 2, XRING)
                dve.wait_ge(out_done, batch.count(TILES, t + 1))
                dve.wait_ge(xb_made, batch.count(HALVES, t // 2 + 1))
                if batch.has(TILES, t - YRING, ALL_TILES):
                    dve.wait_ge(y_stored[t % YRING], batch.count(DMA, DMA * (t // TILES + 1)))
                product = LAST_OUT if bank is None else mi_ps[:, bank, 0:C]
                v.tensor_tensor(y_sb[:, t % YRING], product, x_nat[:, slot, t % 2], ALU.add).then_inc(y_made, 1)

            def slot(batch, u):
                s, j = divmod(u, GROUPS)
                par, n = (s - 1) % 2, batch.count(TILES, s)
                par2, n2 = s % 2, batch.count(TILES, s - 1)
                before, before2 = batch.has(TILES, s - 1, ALL_TILES), batch.has(TILES, s - 2, ALL_TILES)
                if batch.has(UNITS, u + LEAD, ALL_UNITS):
                    maxima(batch, u + LEAD)
                if j == 0 and before2:
                    dve.wait_ge(ipmax_made, n2)
                    v.tensor_tensor(ipd[:, par2], fused[:, par2], ipmax[:, par2].unsqueeze(2).to_broadcast([P, HEADS, NIP]),
                                    ALU.subtract).then_inc(ipd_made, 1)
                if j == 1 and before2:
                    dve.wait_ge(ipe_made, n2)
                    v.tensor_reduce(ipsum[:, par2], ipe[:, par2], AX_X, ALU.add).then_inc(ipsum_made, 1)
                if j == 2 and before2:
                    dve.wait_ge(ipsum_made, n2)
                    v.reciprocal(iprec[:, par2], ipsum[:, par2]).then_inc(iprec_made, 1)
                if j == 2 and before:
                    dve.wait_ge(fin_copied, batch.count(UNITS, GROUPS * s))
                    ssum = fin[:, par, :, FINW - 1]
                    v.reciprocal(rsum[:, par], ssum).then_inc(rsum_made, 1)
                    v.scalar_tensor_tensor(out=guard[:, par], in0=ssum, scalar=EPS * EPS, in1=ssum,
                                           op0=ALU.mult, op1=ALU.mult).then_inc(guard_made, 1)
                kind, m, h, t = misc_task(batch, u - 2)
                if kind == "o":
                    add_residual(batch, misc_bank(batch, h, "o", m), t)
                kind, m, h, t = misc_task(batch, u - 1)
                if kind == "x" and m == 1:
                    x_low(batch, h + 1, m)
                if batch.has(UNITS, u - 1, ALL_UNITS):
                    quadratic(batch, u - 1)
                if j == 2 and before:
                    dve.wait_ge(guard_made, n)
                    v.tensor_tensor(quadc[:, par], quad[:, par], guard[:, par], ALU.max).then_inc(quadc_made, 1)
                if j == 4 and before:
                    dve.wait_ge(fused_made, n)
                    v.tensor_reduce(ipmax[:, par], fused[:, par], AX_X, ALU.max).then_inc(ipmax_made, 1)
                kind, m, h, t = misc_task(batch, u - 1)
                if kind == "x" and m == 0:
                    x_low(batch, h + 1, m)
                if kind == "q":
                    q_low(batch, h + 1, m)
                if batch.number == 0 and 0 <= u - U_SLOT - 1 < B:
                    k = u - U_SLOT - 1
                    dve.wait_ge(u_hi_made, k + 1)
                    v.tensor_tensor(u_all[0:IPROWS, k, 1], u_nat[0:IPROWS, k], u_all[0:IPROWS, k, 0].bitcast(F32),
                                    ALU.subtract).then_inc(u_lo_made, 1)
                if kind == "at":
                    attnT_lows(batch, misc_bank(batch, h, "at", m), t)

            def body(batch):
                for u in range(UNITS):
                    slot(batch, u)

            def drain(batch):
                for u in range(2 * GROUPS - 2):
                    slot(batch, u)
                dve.wait_ge(last_hi, 1)
                v.tensor_tensor(last_attnT_low[:, 0:2 * P], LAST_ATTN[:, 0:2 * P], last_attnT[:, 0:2 * P].bitcast(F32), ALU.subtract)
                v.tensor_tensor(last_attnT[64:P, 2 * P:3 * P], LAST_ATTN[0:64, 2 * P:3 * P], last_attnT[0:64, 2 * P:3 * P].bitcast(F32),
                                ALU.subtract).then_inc(last_lo, 1)
                slot(batch, 2 * GROUPS - 2)
                dve.wait_ge(last_hi, 2)
                v.tensor_tensor(last_attnT_low[0:IPROWS, 2 * P:3 * P], LAST_IP[0:IPROWS],
                                last_attnT[0:IPROWS, 3 * P:4 * P].bitcast(F32), ALU.subtract).then_inc(last_lo, 1)
                add_residual(batch, None, -1)

            run_batches(dve, body, body, drain)

        @block.tensor
        def _(pe):
            mm, tr = nc.tensor.matmul, nc.tensor.transpose

            def x_transposes(batch, half, n):
                slot, use = batch.slot(HALVES, half, XRING)
                if n == 0:
                    pe.wait_ge(in_x[slot], use * DMA + DMA)
                before = bank_released(batch, half - 1, "x", n)
                if before:
                    pe.wait_ge(*before)
                ps = mi_ps[:, misc_bank(batch, half - 1, "x", n), :]
                for t in range(2):
                    if n == 0:
                        for c in range(2):
                            last = tr(ps[:, HALF * c + P * t:HALF * c + P * t + P], x_nat[:, slot, t, P * c:P * c + P], ident[:])
                    else:
                        last = tr(ps[:, P * t:P * t + P], x_nat[:, slot, t, C - P:C], ident[:])
                last.then_inc(xT_done, 1)

            def q_project(batch, half, m):
                if m == 0:
                    pe.wait_ge(xT_lo, batch.count(2 * HALVES, 2 * half + 2))
                before = bank_released(batch, half - 1, "q", m)
                if before:
                    pe.wait_ge(*before)
                ps = mi_ps[0:QROWS[m], misc_bank(batch, half - 1, "q", m), 0:HALF]
                cols = slice(P * m, P * m + QROWS[m])
                steps = [(wq_hi[:, c, cols], xh[:, c, :]) for c in range(3)]
                steps += [(wq_lo[:, c, cols], xh[:, c, :]) for c in range(3)]
                steps += [(wq_hi[:, c, cols], xl[:, c, :]) for c in range(2)]
                for n, (w, xx) in enumerate(steps):
                    last = mm(ps, w, xx, start=n == 0, stop=n == len(steps) - 1)
                last.then_inc(q_done, 1)

            def scores(batch, u):
                s, c = divmod(u % UNITS, GROUPS)
                parity = (batch.parity + u // UNITS) % 2
                half = u // UNITS * HALVES + s // 2
                if batch.has(UNITS, u - 2, ALL_UNITS):
                    pe.wait_ge(exp_done, batch.count(UNITS, u - 1))
                if s == 0:
                    pe.wait_ge(km_made, batch.count(KM_STEPS, KM_STEPS * (u // UNITS) + c + 1))
                if s % 2 == 0 and c % 2 == 0:
                    pe.wait_ge(q_lo, batch.count(3 * HALVES, 3 * half + c // 2 + 1))
                q = qs[:, half % 2, c, P * (s % 2):P * (s % 2) + P]
                for part in range(2):
                    last = mm(sc_ps[:, u % 2, 0:GROUP * TOK], q, km[:, parity, c, part, :], start=part == 0, stop=part == 1)
                last.then_inc(scores_done, 1)

            def e_transposes(batch, u):
                pe.wait_ge(exp_done, batch.count(UNITS, u + 1))
                if batch.has(UNITS, u - 2, ALL_UNITS):
                    pe.wait_ge(eT_copied, batch.count(UNITS, u - 1))
                for r in range(2):
                    last = tr(et_ps[:, u % 2, P * r:P * r + P], e_sb[:, u % ERING, P * r:P * r + P], ident[:])
                last.then_inc(eT_done, 1)

            def table_products(batch, u):
                s, c = divmod(u, GROUPS)
                pe.wait_ge(eT_copied, batch.count(UNITS, u + 1))
                if batch.has(UNITS, u - 2, ALL_UNITS):
                    pe.wait_ge(fin_copied, batch.count(UNITS, u - 1))
                if u == 0:
                    pe.wait_ge(tab_made, batch.count(GV_STEPS, GV_STEPS))
                for r in range(2):
                    h = GROUP * c + 2 * r
                    last = mm(gv_ps[:, u % 2, 2 * TABW * r:2 * TABW * r + 2 * TABW], eT[:, u % TRING, P * r:P * r + P],
                              tab[:, batch.parity, h:h + 2, :].rearrange("p h w -> p (h w)"), start=True, stop=True)
                last.then_inc(gv_done, 1)

            def attn_transposes(batch, h, n, t):
                par = t % 2
                pe.wait_ge(attn_made, batch.count(TILES, t + 1))
                pe.wait_ge(pip_made, batch.count(TILES, t + 1))
                before = bank_released(batch, h, "at", n)
                if before:
                    pe.wait_ge(*before)
                ps = mi_ps[:, misc_bank(batch, h, "at", n), :]
                for c in range(QC):
                    tr(ps[0:QROWS[c], P * c:P * c + P], attn[:, par, P * c:P * c + QROWS[c]], ident[:])
                tr(ps[0:IPROWS, 3 * P:4 * P], pip[:, par].rearrange("p h n -> p (h n)"), ident[:]).then_inc(attnT_done, 1)

            def out_project(batch, h, n, t, part):
                ps = mi_ps[:, misc_bank(batch, h, "o", n), 0:C]
                if part == 0:
                    pe.wait_ge(attnT_lo, batch.count(TILES, t + 1))
                    before = bank_released(batch, h, "o", n)
                    if before:
                        pe.wait_ge(*before)
                steps = out_steps(batch, t, attnT, attnT_low)
                for n in (range(6) if part == 0 else range(6, len(steps))):
                    last = mm(ps, steps[n][0], steps[n][1], start=n == 0, stop=n == len(steps) - 1)
                if part == 1:
                    last.then_inc(out_done, 1)

            def out_steps(batch, t, high, low):
                steps = [(high[:, P * c:P * c + P], wo_parts[:, n, c, :]) for c in range(3) for n in range(2)]
                steps += [(low[:, P * c:P * c + P], wo_parts[:, 0, c, :]) for c in range(2)]
                ip_hi, ip_lo = high[0:IPROWS, 3 * P:4 * P], low[0:IPROWS, 2 * P:3 * P]
                b = batch.count(1, t // TILES)
                u_row = (lambda n: u_all[0:IPROWS, b, n, :]) if isinstance(b, int) else (
                    lambda n: u_all[0:IPROWS, bass.ds(b, 1), n, :].rearrange("p b c -> p (b c)"))
                steps += [(ip_hi, u_row(0)), (ip_hi, u_row(1)), (ip_lo, u_row(0))]
                return steps

            def last_attn_transposes():
                par = (TILES - 1) % 2
                pe.wait_ge(attn_made, B * TILES)
                for c in range(QC):
                    last = tr(LAST_ATTN[0:QROWS[c], P * c:P * c + P], attn[:, par, P * c:P * c + QROWS[c]], ident[:])
                last.then_inc(last_done, 1)

            def last_products(batch):
                n, par = B * TILES, (TILES - 1) % 2
                steps = out_steps(batch, -1, last_attnT, last_attnT_low)
                pe.wait_ge(last_lo, 1)
                for k in range(len(steps) - 3):
                    mm(LAST_OUT, steps[k][0], steps[k][1], start=k == 0, stop=False)
                pe.wait_ge(pip_made, n)
                tr(LAST_IP[0:IPROWS], pip[:, par].rearrange("p h n -> p (h n)"), ident[:]).then_inc(last_done, 1)
                pe.wait_ge(last_lo, 2)
                for k in range(len(steps) - 3, len(steps)):
                    last = mm(LAST_OUT, steps[k][0], steps[k][1], start=False, stop=k == len(steps) - 1)
                last.then_inc(out_done, 1)

            pe.wait_ge(ident_made, 1)
            for q in range(PAIRS):
                pe.wait_ge(in_ctx[q], DMA)
                for c in range(EC):
                    last = tr(BANKS[q][:, P * c:P * c + P], ctx_nat[:, q, P * c:P * c + P], ident[:])
                last.then_inc(pre_ctxT, 1)
            pe.wait_ge(ipn_made, 1)
            for c in range(EC):
                last = tr(BANKS[5][:, 32 * c:32 * c + 32], ipn[:, P * c:P * c + P], ident[0:B * NIP, 0:B * NIP])
            last.then_inc(pre_ipn, 1)
            x_transposes(Batch(0), 0, 0)
            x_transposes(Batch(0), 0, 1)
            pe.wait_ge(ctxM_made, 1)
            for q in range(PAIRS):
                pe.wait_ge(ctxM_text, q + 1)
                for c in range(EC):
                    last = mm(BANKS[4][:, P * q:P * q + P], ctxT[:, c, P * q:P * q + P], ctxM[:, c, P * q:P * q + P],
                              start=c == 0, stop=c == EC - 1)
            last.then_inc(pre_g, 1)
            pe.wait_ge(wv_hi_made, 1)

            def v_product(q, bank):
                tokens = slice(P * q, P * q + P)
                steps = [(cc[:, c, tokens], ww[:, c, :]) for cc, ww in ((ctx_hi, wv_hi), (ctx_lo, wv_hi), (ctx_hi, wv_lo))
                         for c in range(EC)]
                for n, (cc, ww) in enumerate(steps):
                    if q == 0 and n == EC:
                        pe.wait_ge(ctx_lo_made, 1)
                    if q == 0 and n == 2 * EC:
                        pe.wait_ge(wv_lo_made, 1)
                    last = mm(bank[:, 0:C], cc, ww, start=n == 0, stop=n == len(steps) - 1)
                last.then_inc(pre_v, 1)

            for q in range(PAIRS - 1):
                v_product(q, BANKS[q])
            by_batch = ctxT.rearrange("p c (b t) -> p c b t", t=TOK)
            pe.wait_ge(wk_lo_made, 1)
            pe.wait_ge(in_wkip, DMA)
            text_hi, text_lo = (cc.rearrange("p c (b t) -> p c b t", t=TOK)[:, :, :, 0:T] for cc in (ctx_hi, ctx_lo[:]))
            for m in range(QC):
                if m == 1:
                    pe.wait_ge(g_copied, 2)
                if m == 2:
                    pe.wait_ge(v_copied, PAIRS - 1)
                ps = BANKS[K_BANKS[m]][0:QROWS[m], :].rearrange("p (b t) -> p b t", t=TOK)
                cols = slice(P * m, P * m + QROWS[m])
                steps = [(ww[:, c, cols], cc[:, c]) for ww, cc in ((wk_hi, text_hi), (wk_lo, text_hi), (wk_hi, text_lo))
                         for c in range(EC)]
                for n, (ww, cc) in enumerate(steps):
                    mm(ps[:, :, 0:T], ww, cc, start=n == 0, stop=n == len(steps) - 1)
                for c in range(EC):
                    last = mm(ps[:, :, T:TOK], wkip[:, c, P * m:P * m + QROWS[m]], by_batch[:, c, :, T:TOK],
                              start=c == 0, stop=c == EC - 1)
                last.then_inc(pre_k, 1)
                if m == 0:
                    pe.wait_ge(wq_lo_made, 1)
                q_project(Batch(0), 0, m)
            scores(Batch(0), 0)
            scores(Batch(0), 1)
            pe.wait_ge(in_wvip, DMA)
            pe.wait_ge(k_lo, 4)
            for m in range(QC):
                for c in range(EC):
                    last = mm(BANKS[5][0:QROWS[m], 32 * m:32 * m + 32].rearrange("p (b n) -> p b n", n=NIP),
                              wvip[:, c, P * m:P * m + QROWS[m]], by_batch[:, c, :, T:TOK], start=c == 0, stop=c == EC - 1)
            last.then_inc(pre_vip, 1)
            pe.wait_ge(q_lo, 2)
            v_product(PAIRS - 1, mi_ps[:, 1, :])
            pe.wait_ge(zeros_made, 6)
            e_transposes(Batch(0), 0)
            pe.wait_ge(vip_made, QC)
            pe.wait_ge(in_wo, 3 * DMA)
            pe.wait_ge(k_lo, 2 * GROUPS)
            for n in range(5):
                m, part = (n // 2, n % 2) if n < 4 else (2, 0)
                if n > 2:
                    pe.wait_ge(u_copied, n - 2)
                mm(BANKS[U_BANKS[n]][:, 0:C], vip_bd[0:QROWS[m], m, P * part:P * part + P], wo[0:QROWS[m], m, :],
                   start=True, stop=True).then_inc(pre_u, 1)
                if n == 2:
                    scores(Batch(0), 2)
            pe.wait_ge(u_copied, 5)
            e_transposes(Batch(0), 1)
            scores(Batch(0), 3)

            def slot(batch, u):
                if batch.has(UNITS, u + TLEAD, ALL_UNITS):
                    e_transposes(batch, u + TLEAD)
                if batch.has(UNITS, u + SLEAD, ALL_UNITS):
                    scores(batch, u + SLEAD)
                kind, n, h, t = misc_task(batch, u - 1)
                if kind == "o":
                    if batch.number == 0 and t == 0:
                        pe.wait_ge(u_lo_made, 1)
                        pe.wait_ge(wo_lo_made, 1)
                    out_project(batch, h, n, t, 1)
                kind, n, h, t = misc_task(batch, u)
                early = (kind, n) == ("q", 0)
                if early and batch.has(UNITS, u, ALL_UNITS):
                    table_products(batch, u)
                if kind == "x":
                    x_transposes(batch, h + 1, n)
                if kind == "q":
                    q_project(batch, h + 1, n)
                if kind == "at":
                    attn_transposes(batch, h, n, t)
                if kind == "o":
                    out_project(batch, h, n, t, 0)
                if not early and batch.has(UNITS, u, ALL_UNITS):
                    table_products(batch, u)

            def body(batch):
                for u in range(UNITS):
                    slot(batch, u)

            def drain(batch):
                for u in range(2 * GROUPS - 2):
                    if u == GROUPS + 1:
                        last_attn_transposes()
                    slot(batch, u)
                last_products(batch)

            run_batches(pe, body, body, drain)


_INS = ["x", "ctx_2048", "fside_S_0", "L0_xattn_W_q", "L0_xattn_W_k", "L0_xattn_W_v",
        "L0_xattn_W_k_ip", "L0_xattn_W_v_ip", "L0_xattn_W_out", "L0_xattn_b_out"]


def kernel(**inputs):
    import numpy as _np
    import concourse.bacc as _bacc
    from concourse.bass_utils import run_bass_kernel_spmd as _run

    nc = _bacc.Bacc("TRN2", target_bir_lowering=False, num_devices=1)
    arrays, args = {}, []
    for name in _INS:
        a = _np.ascontiguousarray(inputs[name])
        arrays[f"in_{name}"] = a
        args.append(nc.dram_tensor(f"in_{name}", a.shape, mybir.dt.from_np(a.dtype), kind="ExternalInput").ap())
    out = nc.dram_tensor("out", inputs["x"].shape, F32, kind="ExternalOutput").ap()
    with nc.allow_non_contiguous_dma(reason="the spatial mask is 512 numbers, one column a tile"):
        xattn_kernel(nc, *args, out)
    r = _run(nc, [arrays], core_ids=[0])
    return r.results[0]["out"]
```
